# Optimizing a Trainium2 kernel written in Bass

```python
import numpy as np
import jax
import jax.numpy as jnp

def _softmax(x, axis=-1):
    return jax.nn.softmax(x, axis=axis)

def _gelu(x):
    return jax.nn.gelu(x, approximate=True)

def _silu(x):
    return jax.nn.silu(x)

def _sigmoid(x):
    return jax.nn.sigmoid(x)

def _layernorm(x, axis=-1, eps=1e-05):
    m = jnp.mean(x, axis=axis, keepdims=True)
    v = jnp.var(x, axis=axis, keepdims=True)
    return (x - m) / jnp.sqrt(v + eps)

def _scatter_add(tgt, idx, src, axis=0):
    return tgt.at[idx].add(src)

def _segment_sum(src, seg, n):
    return jax.ops.segment_sum(src, seg, n)
kernel_name = 'mk_conv_preact_d2_conv_nhwc384_r2_4deea0'

def setup_inputs(seed: int=0):
    np.random.seed(seed)
    _w = jnp.asarray

    def _rec_inputs():
        import jax
        import jax.numpy as jnp
        _gk = jax.random.key(seed)
        x = -0.000357 + 1 * jax.random.normal(jax.random.fold_in(_gk, 1), (16, 56, 56, 192), jnp.float32)
        return x
    x = _rec_inputs()

    def _L0_conv_setup():
        import jax, jax.numpy as jnp
        import numpy as np
        DIM = 192
        HEADS = 6
        K = 3
        key = jax.random.key(seed)
        ks = jax.random.split(key, 7)
        B, H, W, C = (16, 56, 56, DIM)
        sc = 1.0 / np.sqrt(C)
        return {'x_map': jax.random.normal(ks[0], (B, H, W, C), dtype=jnp.float32), 'W_attn': jax.random.normal(ks[1], (C, HEADS * K * K), dtype=jnp.float32) * sc, 'b_attn': jax.random.normal(ks[2], (HEADS * K * K,), dtype=jnp.float32) * 0.02, 'W_v': jax.random.normal(ks[3], (C, C), dtype=jnp.float32) * sc, 'b_v': jax.random.normal(ks[4], (C,), dtype=jnp.float32) * 0.02, 'W_proj': jax.random.normal(ks[5], (C, C), dtype=jnp.float32) * sc, 'b_proj': jax.random.normal(ks[6], (C,), dtype=jnp.float32) * 0.02}
    _L0_conv_all = _L0_conv_setup()
    _L0_conv_in = {k: v for k, v in _L0_conv_all.items() if k in ('W_attn', 'b_attn', 'W_v', 'b_v', 'W_proj', 'b_proj')}
    del _L0_conv_all

    def _L1_conv_setup():
        import jax, jax.numpy as jnp
        import numpy as np
        WS = (7, 7)
        SS = (3, 3)
        NH = 12
        C = 192

        def _rel_pos_index(ws):
            ch = np.arange(ws[0])
            cw = np.arange(ws[1])
            coords = np.stack(np.meshgrid(ch, cw, indexing='ij'))
            cf = coords.reshape(2, -1)
            rel = cf[:, :, None] - cf[:, None, :]
            rel = rel.transpose(1, 2, 0)
            rel[:, :, 0] += ws[0] - 1
            rel[:, :, 1] += ws[1] - 1
            rel[:, :, 0] *= 2 * ws[1] - 1
            return rel.sum(-1).reshape(-1)

        def _shift_mask(pad_h, pad_w, ws, ss):
            m = np.zeros((pad_h, pad_w), dtype=np.float32)
            h_sl = [(0, pad_h - ws[0]), (pad_h - ws[0], pad_h - ss[0]), (pad_h - ss[0], pad_h)]
            w_sl = [(0, pad_w - ws[1]), (pad_w - ws[1], pad_w - ss[1]), (pad_w - ss[1], pad_w)]
            cnt = 0
            for h0, h1 in h_sl:
                for w0, w1 in w_sl:
                    m[h0:h1, w0:w1] = cnt
                    cnt += 1
            m = m.reshape(pad_h // ws[0], ws[0], pad_w // ws[1], ws[1])
            m = m.transpose(0, 2, 1, 3).reshape(-1, ws[0] * ws[1])
            diff = m[:, None, :] - m[:, :, None]
            return np.where(diff != 0, -100.0, 0.0).astype(np.float32)
        key = jax.random.key(seed)
        ks = jax.random.split(key, 6)
        B, H, W = (32, 56, 56)
        nbias = (2 * WS[0] - 1) * (2 * WS[1] - 1)
        return {'x': jax.random.normal(ks[0], (B, H, W, C), jnp.float32), 'qkv_weight': jax.random.normal(ks[1], (3 * C, C), jnp.float32) * 0.02, 'qkv_bias': jnp.zeros((3 * C,), jnp.float32), 'proj_weight': jax.random.normal(ks[2], (C, C), jnp.float32) * 0.02, 'proj_bias': jnp.zeros((C,), jnp.float32), 'rel_pos_bias_table': jax.random.normal(ks[3], (nbias, NH), jnp.float32) * 0.02}
    _L1_conv_all = _L1_conv_setup()
    _L1_conv_in = {k: v for k, v in _L1_conv_all.items() if k in ('qkv_weight', 'qkv_bias', 'proj_weight', 'proj_bias', 'rel_pos_bias_table')}
    del _L1_conv_all
    return {'x': x, 'L0_conv_W_attn': _L0_conv_in['W_attn'], 'L0_conv_b_attn': _L0_conv_in['b_attn'], 'L0_conv_W_v': _L0_conv_in['W_v'], 'L0_conv_b_v': _L0_conv_in['b_v'], 'L0_conv_W_proj': _L0_conv_in['W_proj'], 'L0_conv_b_proj': _L0_conv_in['b_proj'], 'L1_conv_qkv_weight': _L1_conv_in['qkv_weight'], 'L1_conv_qkv_bias': _L1_conv_in['qkv_bias'], 'L1_conv_proj_weight': _L1_conv_in['proj_weight'], 'L1_conv_proj_bias': _L1_conv_in['proj_bias'], 'L1_conv_rel_pos_bias_table': _L1_conv_in['rel_pos_bias_table']}

def reference(x, L0_conv_W_attn, L0_conv_b_attn, L0_conv_W_v, L0_conv_b_v, L0_conv_W_proj, L0_conv_b_proj, L1_conv_qkv_weight, L1_conv_qkv_bias, L1_conv_proj_weight, L1_conv_proj_bias, L1_conv_rel_pos_bias_table):
    import jax
    import jax.numpy as jnp

    def _L0_conv_ref(x_map, W_attn, b_attn, W_v, b_v, W_proj, b_proj):
        import jax, jax.numpy as jnp
        import numpy as np
        DIM = 192
        HEADS = 6
        K = 3
        B, H, W, C = x_map.shape
        k, heads = (K, HEADS)
        hd = C // heads
        pad = k // 2
        a = x_map @ W_attn + b_attn
        a = jax.nn.softmax(a.reshape(B, H * W, heads, k * k), axis=-1)
        v = x_map @ W_v + b_v
        vp = jnp.pad(v, ((0, 0), (pad, pad), (pad, pad), (0, 0)))
        patches = jnp.stack([vp[:, i:i + H, j:j + W, :] for i in range(k) for j in range(k)], axis=3)
        patches = patches.reshape(B, H * W, k * k, heads, hd)
        y = jnp.einsum('bpKhd,bphK->bphd', patches, a)
        y = y.reshape(B, H, W, C)
        return y @ W_proj + b_proj

    def _L1_conv_ref(x, qkv_weight, qkv_bias, proj_weight, proj_bias, rel_pos_bias_table):
        import jax, jax.numpy as jnp
        import numpy as np
        WS = (7, 7)
        SS = (3, 3)
        NH = 12
        C = 192

        def _rel_pos_index(ws):
            ch = np.arange(ws[0])
            cw = np.arange(ws[1])
            coords = np.stack(np.meshgrid(ch, cw, indexing='ij'))
            cf = coords.reshape(2, -1)
            rel = cf[:, :, None] - cf[:, None, :]
            rel = rel.transpose(1, 2, 0)
            rel[:, :, 0] += ws[0] - 1
            rel[:, :, 1] += ws[1] - 1
            rel[:, :, 0] *= 2 * ws[1] - 1
            return rel.sum(-1).reshape(-1)

        def _shift_mask(pad_h, pad_w, ws, ss):
            m = np.zeros((pad_h, pad_w), dtype=np.float32)
            h_sl = [(0, pad_h - ws[0]), (pad_h - ws[0], pad_h - ss[0]), (pad_h - ss[0], pad_h)]
            w_sl = [(0, pad_w - ws[1]), (pad_w - ws[1], pad_w - ss[1]), (pad_w - ss[1], pad_w)]
            cnt = 0
            for h0, h1 in h_sl:
                for w0, w1 in w_sl:
                    m[h0:h1, w0:w1] = cnt
                    cnt += 1
            m = m.reshape(pad_h // ws[0], ws[0], pad_w // ws[1], ws[1])
            m = m.transpose(0, 2, 1, 3).reshape(-1, ws[0] * ws[1])
            diff = m[:, None, :] - m[:, :, None]
            return np.where(diff != 0, -100.0, 0.0).astype(np.float32)
        b, h, w, c = x.shape
        n = WS[0] * WS[1]
        hd = c // NH
        pad_h, pad_w = (h, w)
        nW = pad_h // WS[0] * (pad_w // WS[1])
        idx = jnp.asarray(_rel_pos_index(WS))
        rpb = rel_pos_bias_table[idx].reshape(n, n, NH).transpose(2, 0, 1)
        xs = jnp.roll(x, shift=(-SS[0], -SS[1]), axis=(1, 2))
        xw = xs.reshape(b, pad_h // WS[0], WS[0], pad_w // WS[1], WS[1], c)
        xw = xw.transpose(0, 1, 3, 2, 4, 5).reshape(b * nW, n, c)
        qkv = xw @ qkv_weight.T + qkv_bias
        qkv = qkv.reshape(b * nW, n, 3, NH, hd).transpose(2, 0, 3, 1, 4)
        q, k, v = (qkv[0], qkv[1], qkv[2])
        attn = jnp.einsum('wmqd,wmkd->wmqk', q * hd ** (-0.5), k)
        attn = attn + rpb[None]
        mask = jnp.asarray(_shift_mask(pad_h, pad_w, WS, SS))
        attn = attn.reshape(b, nW, NH, n, n) + mask[None, :, None]
        attn = attn.reshape(b * nW, NH, n, n)
        attn = jax.nn.softmax(attn, axis=-1)
        out = jnp.einsum('wmqk,wmkd->wqmd', attn, v).reshape(b * nW, n, c)
        out = out @ proj_weight.T + proj_bias
        out = out.reshape(b, pad_h // WS[0], pad_w // WS[1], WS[0], WS[1], c)
        out = out.transpose(0, 1, 3, 2, 4, 5).reshape(b, pad_h, pad_w, c)
        out = jnp.roll(out, shift=(SS[0], SS[1]), axis=(1, 2))
        return out

    def _gn(v, G=32, eps=1e-05):
        B_, H_, W_, C_ = v.shape
        g = v.reshape(B_, H_, W_, G, C_ // G)
        m = jnp.mean(g, axis=(1, 2, 4), keepdims=True)
        s = jnp.var(g, axis=(1, 2, 4), keepdims=True)
        return ((g - m) / jnp.sqrt(s + eps)).reshape(v.shape)

    def _ln_c(v, eps=1e-06):
        m = jnp.mean(v, axis=-1, keepdims=True)
        s = jnp.var(v, axis=-1, keepdims=True)
        return (v - m) / jnp.sqrt(s + eps)

    def _ln_t(v, eps=1e-05):
        m = jnp.mean(v, axis=-1, keepdims=True)
        s = jnp.var(v, axis=-1, keepdims=True)
        return (v - m) / jnp.sqrt(s + eps)

    def _to_tokens(v):
        B_, H_, W_, C_ = v.shape
        return v.reshape(B_, H_ * W_, C_)

    def _from_tokens(t, like):
        return t.reshape(like.shape)
    x = x + _L0_conv_ref(_gn(x), L0_conv_W_attn, L0_conv_b_attn, L0_conv_W_v, L0_conv_b_v, L0_conv_W_proj, L0_conv_b_proj)
    x = x + _L1_conv_ref(_gn(x), L1_conv_qkv_weight, L1_conv_qkv_bias, L1_conv_proj_weight, L1_conv_proj_bias, L1_conv_rel_pos_bias_table)
    return x

_drawn_inputs = setup_inputs


def setup_inputs(seed=0):
    import zlib

    import numpy as np

    out = dict(_drawn_inputs(seed))
    spreads = {'L1_conv_qkv_bias': (0.0, 0.281), 'L1_conv_proj_bias': (0.0, 0.1)}
    factors = {'L0_conv_b_attn': 8.0,
     'L0_conv_b_v': 2.795,
     'L0_conv_b_proj': 2.988,
     'L1_conv_qkv_weight': 4.194,
     'L1_conv_rel_pos_bias_table': 38.793}
    for name, (base, spread) in spreads.items():
        noise = np.random.default_rng([zlib.crc32(name.encode()), seed]).standard_normal(out[name].shape)
        drawn = base * np.exp(spread * noise) if base else spread * noise
        out[name] = jnp.asarray(drawn.astype(out[name].dtype))
    for name, factor in factors.items():
        out[name] = (out[name] * factor).astype(out[name].dtype)
    return out
```

```python
from contextlib import ExitStack

import numpy as np

import concourse.bass as bass
from concourse import mybir

F32 = mybir.dt.float32
BF16 = mybir.dt.bfloat16
ALU = mybir.AluOpType
ACT = mybir.ActivationFunctionType
AX = mybir.AxisListType

B, H, W, C = 16, 56, 56, 192
HALF = C // 2
EPS = 1e-5
GROUP = C // 32
OHEADS, KK = 6, 9
LOGITS = OHEADS * KK
LP = 66
HK = LOGITS // 2
SPLITS = 3
ROWS = 8
CHUNKS = H // ROWS
CT = ROWS * W
TT = 112
NT = CT // TT
REPS = 2 * KK
PROJECT_SLOTS = (7, 8, 9, 11, 12, 14)
RING = 6
PADD = 6
WS, SHIFT = 7, 3
NH, HD = 12, 16
NW = W // WS
N = WS * WS
RT = NW * N
PAIRS = NW // 2
SLOT = 64
HH = NH // 2
NTAB = 2 * WS - 1
XP = W + SHIFT
ONE = 1
QKV = 8
STEP_TILES = ((0, 1, 2), (3, 4, 5), (6, 7), ())
BDMA = HH * 2


def mixer(nc, x, wa, ba, wv, bv, wp, bp, wqkv, bqkv, wo, bo, table, sel_in, gmat_in, mask_in, out):
    ctx = ExitStack()
    with ctx:
        def sb(name, shape, dt=F32):
            return ctx.enter_context(nc.sbuf_tensor(name, shape, dt))

        def sem(name):
            return ctx.enter_context(nc.semaphore(name))

        ident = sb("ident", [128, 128])
        identb = sb("identb", [128, 128], BF16)
        gmat = sb("gmat", [HALF, HALF])
        self32 = sb("self32", [HK * SPLITS, KK * HALF])
        sel = sb("sel", [HK * SPLITS, KK, HALF], BF16)
        wa_s = sb("wa_s", [HALF, 2, LOGITS])
        ba_s = sb("ba_s", [LOGITS, 1])
        wv_s = sb("wv_s", [HALF, 2, C])
        wp_s = sb("wp_s", [HALF, 2, C])
        bias = sb("bias", [HALF, 7, 2])
        bout = sb("bout", [HALF, 2])
        wt = sb("wt", [HALF, 2, 3 * C])
        wot = sb("wot", [HALF, 2, C])
        eps_s = sb("eps_s", [HALF, 1])
        relb = sb("relb", [128, 4, NH * N])
        junk = sb("junk", [128, 512], BF16)
        xin = sb("xin", [TT, 2, NT, C])
        xa = sb("xa", [HALF, 2, XP, XP])
        vpad = sb("vpad", [HALF, 2, H + 2, W + 2])
        stats = sb("stats", [HALF, 2, CHUNKS, 6])
        fence = sb("fence", [HALF, 1])
        table_t = sb("table_t", [HALF, 1])
        mv = sb("mv", [HALF, 2, 2])
        gdev = sb("gdev", [HALF, 2])
        gmean = sb("gmean", [HALF, 2])
        gsq = sb("gsq", [HALF, 2])
        gstd = sb("gstd", [HALF, 2])
        ga = sb("ga", [HALF, 2])
        gb = sb("gb", [HALF, 2])
        xn = sb("xn", [HALF, 2, CT])
        lg = sb("lg", [LP, CT])
        smx = sb("smx", [TT, NT * OHEADS])
        ssh = sb("ssh", [TT, NT * LOGITS])
        sex = sb("sex", [TT, NT * LOGITS])
        ssum = sb("ssum", [TT, NT * OHEADS])
        srec = sb("srec", [TT, NT * OHEADS])
        sa = sb("sa", [TT, NT * LOGITS])
        srest = sb("srest", [TT, NT * LOGITS])
        asp = sb("asp", [TT, NT * 2, SPLITS, HK], BF16)
        at = sb("at", [HK * SPLITS, 2 * 2 * CT], BF16)
        prod = sb("prod", [HALF, RING, CT])
        ptail = sb("ptail", [HALF, 3, CT])
        psum_p = sb("psum_p", [HALF, CT])
        y0 = sb("y0", [HALF, 2, CT])
        xw = sb("xw", [HALF, 2, 2, RT])
        xr = sb("xr", [HALF, 2, 2, RT])
        qs = sb("qs", [HALF, 2, 2, RT + SLOT - N])
        ks = sb("ks", [HALF, 2, RT])
        kbd = sb("kbd", [HALF, 2, 2, HH, RT // 2])
        vs = sb("vs", [2 * N, PAIRS, 2, C])
        vbd = sb("vbd", [2 * N, 2, NW, C])
        ts_ = sb("ts_", [128, 2, NH * N])
        ps_ = sb("ps_", [128, 2, NH * N])
        mx = sb("mx", [128, 2, NH])
        sm = sb("sm", [128, 2, NH])
        rc = sb("rc", [128, 2, NH])
        pt = sb("pt", [2 * N, 2, NH // 2, 2, N])
        yt = sb("yt", [HALF, 2, 2, RT])
        ot = sb("ot", [TT, PAIRS, C])
        P = ctx.enter_context(nc.psum_tensor("P", [128, 8, 512], F32))
        wn = prod[:, :, :].rearrange("p a b -> p (a b)")[:, 0:6 * C].rearrange("p (a b) -> p a b", a=6)
        wno = ptail[:, 0, 0:2 * C].rearrange("p (a b) -> p a b", a=2)
        rel_raw = ts_[:, 0, :].rearrange("p (k h) -> p k h", h=NH)
        mask_s = ps_[:, 0, 0:4 * N].rearrange("p (v k) -> p v k", v=4)

        consts_in = sem("consts_in"); rel_in = sem("rel_in")
        zeroed = sem("zeroed"); rel_zero = sem("rel_zero"); idents = sem("idents"); w_cast = sem("w_cast")
        w_turned = sem("w_turned"); w_kept = sem("w_kept"); bout_mm = sem("bout_mm"); bout_ok = sem("bout_ok")
        rel_ok = sem("rel_ok"); wscaled = sem("wscaled")
        x_in = [sem("x_in0"), sem("x_in1")]
        x_turned = sem("x_turned"); x_kept = sem("x_kept"); x_stat = sem("x_stat")
        g_agg = sem("g_agg"); g_table = sem("g_table"); g_mean = sem("g_mean"); g_dev = sem("g_dev"); g_sq = sem("g_sq")
        g_var = sem("g_var"); g_std = sem("g_std"); g_rstd = sem("g_rstd"); g_ready = sem("g_ready")
        xn_ok = sem("xn_ok"); l_mm = sem("l_mm"); l_kept = sem("l_kept"); l_turned = sem("l_turned")
        v_mm = sem("v_mm"); v_kept = sem("v_kept")
        s_max = sem("s_max"); s_sub = sem("s_sub"); s_exp = sem("s_exp"); s_sum = sem("s_sum")
        s_rec = sem("s_rec"); s_norm = sem("s_norm"); sp_hi = sem("sp_hi"); sp_rest = sem("sp_rest")
        sp_mid = sem("sp_mid"); sp_low = sem("sp_low"); a_turned = sem("a_turned"); a_kept = sem("a_kept")
        rep_mm = sem("rep_mm"); prod_ok = sem("prod_ok"); tail_ok = sem("tail_ok"); padd_ok = sem("padd_ok")
        o_mm = sem("o_mm"); x1_kept = sem("x1_kept"); x1_stat = sem("x1_stat"); x1_wrap = sem("x1_wrap")
        xw_ok = sem("xw_ok"); xr_ok = sem("xr_ok"); qkv_mm = sem("qkv_mm"); qkv_kept = sem("qkv_kept")
        k_in = [sem("k_in0"), sem("k_in1")]; v_in = sem("v_in")
        sc_mm = sem("sc_mm"); t_add = sem("t_add"); t_max = sem("t_max"); t_sub = sem("t_sub")
        p_exp = sem("p_exp"); p_sum = sem("p_sum"); p_rec = sem("p_rec"); p_norm = sem("p_norm")
        p_turned = sem("p_turned"); p_kept = sem("p_kept"); y_mm = sem("y_mm"); y_kept = sem("y_kept")
        out_mm = sem("out_mm"); res_kept = sem("res_kept"); out_ok = sem("out_ok")
        out_in = [sem(f"out_in{p}") for p in range(PAIRS)]

        counted = [x_turned, g_table, x_kept, x_stat, g_agg, g_mean, g_dev, g_sq, g_var, g_std,
                   g_rstd, g_ready, xn_ok, l_mm, l_kept, l_turned, v_mm, v_kept, s_max,
                   s_sub, s_exp, s_sum, s_rec, s_norm, sp_hi, sp_rest, sp_mid, sp_low,
                   a_turned, a_kept, rep_mm, prod_ok, tail_ok, padd_ok, o_mm, x1_kept, x1_stat,
                   x1_wrap, xw_ok, xr_ok, qkv_mm, qkv_kept, v_in, sc_mm, t_add, t_max,
                   t_sub, p_exp, p_sum, p_rec, p_norm, p_turned, p_kept, y_mm, y_kept,
                   out_mm, res_kept, out_ok, *x_in, *k_in, *out_in]

        block = ctx.enter_context(nc.Block())

        def x_load(sp, i, c, slot):
            src = x[bass.ds(i * (H * W) + c * CT, CT), :].rearrange("(t p) n -> p t n", p=TT)
            return sp.dma_start(xin[:, slot, :, :], src)

        NCONST = 20

        @block.sync
        def _(sp):
            def load_bias(j, v):
                for h in range(2):
                    sp.dma_start(bias[:, j, h:h + 1], v[h * HALF:(h + 1) * HALF].rearrange("(p a) -> p a", a=1)
                                 ).then_inc(consts_in, 16)

            sp.dma_start(wn, wqkv.rearrange("(b p) n -> p b n", p=HALF)).then_inc(consts_in, 16)
            sp.dma_start(wno, wo.rearrange("(b p) n -> p b n", p=HALF)).then_inc(consts_in, 16)
            sp.dma_start(wa_s[:], wa.rearrange("(h p) n -> p h n", p=HALF)).then_inc(consts_in, 16)
            sp.dma_start(wv_s[:], wv.rearrange("(h p) n -> p h n", p=HALF)).then_inc(consts_in, 16)
            sp.dma_start(wp_s[:], wp.rearrange("(h p) n -> p h n", p=HALF)).then_inc(consts_in, 16)
            sp.dma_start(gmat[:], gmat_in).then_inc(consts_in, 16)
            sp.dma_start(self32[:], sel_in).then_inc(consts_in, 16)
            sp.dma_start(ba_s[:], ba.rearrange("(p a) -> p a", a=1)).then_inc(consts_in, 16)
            load_bias(0, bv)
            load_bias(1, bp)
            for j in range(3):
                load_bias(2 + j, bqkv[j * C:(j + 1) * C])
            load_bias(5, bo)
            sp.dma_start(mask_s, mask_in).then_inc(rel_in, 16)
            sp.wait_ge(rel_zero, 1)
            for s in range(2):
                for r in range(WS):
                    p0 = s * SLOT + r * WS
                    src = bass.AP(tensor=table.tensor, offset=table.offset + r * NTAB * NH,
                                  ap=[[NH, WS], [NTAB * NH, WS], [1, WS * NH]])
                    dst = ts_[p0:p0 + WS, 0, :].rearrange("p (a b) -> p a b", a=WS)
                    sp.dma_start(dst, src).then_inc(rel_in, 16)
            for c in range(2):
                x_load(sp, 0, c, c).then_inc(x_in[c], 16)

            with sp.Fori(0, B) as i:
                for c in range(2, CHUNKS):
                    sp.wait_ge(x_turned, ONE + 2 * (CHUNKS * i + c - 1))
                    x_load(sp, i, c, c % 2).then_inc(x_in[c % 2], 16)

                def spread_k(w, d):
                    R = NW * i + w
                    made = sp.to_reg(ONE + QKV * R + 2)
                    used = sp.to_reg(ONE + 2 * PAIRS * R
                                     + (0 if isinstance(w, int) and w == 0 else 4 * d + 4 - 2 * PAIRS))
                    sp.wait_ge(qkv_kept, made)
                    sp.wait_ge(sc_mm, used)
                    for h in range(2):
                        for m in range(HH):
                            sp.dma_start(kbd[HD * m:HD * m + HD, d, h, m, :],
                                         ks[HD * m:HD * m + HD, h, d * (RT // 2):(d + 1) * (RT // 2)]
                                         ).then_inc(k_in[d], 16)

                def spread_v(w, par):
                    R = NW * i + w
                    made = sp.to_reg(ONE + QKV * (R + 1))
                    used = sp.to_reg(ONE + (PAIRS * NW * i if isinstance(w, int) and w < 2 else PAIRS * (R - 1)))
                    sp.wait_ge(qkv_kept, made)
                    sp.wait_ge(y_mm, used)
                    for s in range(2):
                        for e in range(2):
                            sp.dma_start(vbd[N * e:N * e + N, par, s::2, :],
                                         vs[N * s:N * s + N, :, e, :]).then_inc(v_in, 16)

                def store(w, p):
                    R = NW * i + w
                    sp.wait_ge(out_ok, ONE + PAIRS * R + p + 1)
                    row = WS * w + SHIFT + 2 * p
                    if isinstance(w, int):
                        row %= H
                    n = min(TT, RT - TT * p)
                    sp.dma_start(out[bass.ds(i * (H * W) + row * W, n), :], ot[0:n, p, :]
                                 ).then_inc(out_in[p], 16)

                def row_dmas(w, par, first, last):
                    if not last:
                        spread_k(w + 1, 0)
                    if not first:
                        store(w - 1, 0)
                    if not last:
                        spread_k(w + 1, 1)
                    if not first:
                        store(w - 1, 1)
                    if not last:
                        spread_v(w + 1, 1 - par)
                    if not first:
                        for p in range(2, PAIRS):
                            store(w - 1, p)

                spread_k(0, 0)
                spread_k(0, 1)
                spread_v(0, 0)
                row_dmas(0, 0, True, False)
                with sp.Fori(0, NW // 2 - 1) as u:
                    row_dmas(2 * u + 1, 1, False, False)
                    row_dmas(2 * u + 2, 0, False, False)
                row_dmas(NW - 1, 1, False, True)
                for p in range(PAIRS):
                    store(NW - 1, p)
                after = sp.snap((i + 1) % B)
                for c in range(2):
                    sp.wait_ge(x_turned, ONE + 2 * CHUNKS * (i + 1))
                    x_load(sp, after, c, c).then_inc(x_in[c], 16)
            for p in range(PAIRS):
                sp.wait_ge(out_in[p], ONE + 16 * B * NW)
            sp.wait_ge(x_in[0], ONE + 16 * (B * 4 + 1))
            sp.wait_ge(x_in[1], ONE + 16 * (B * 3 + 1))

        @block.tensor
        def _(pe):
            mm, turn = nc.tensor.matmul, nc.tensor.transpose
            pe.wait_ge(idents, 4)
            pe.wait_ge(consts_in, 16 * NCONST)
            for b in range(8):
                src = wn[:, b, :] if b < 6 else wno[:, b - 6, :]
                if b >= 4:
                    pe.wait_ge(w_kept, b - 3)
                for h in range(2):
                    last = turn(P[0:HALF, b % 4, h * HALF:(h + 1) * HALF], src[:, h * HALF:(h + 1) * HALF],
                                ident[0:HALF, 0:HALF])
                last.then_inc(w_turned, 1)
            pe.wait_ge(w_kept, 8)
            for m in range(2):
                for h in range(2):
                    last = mm(P[0:HALF, 4, m:m + 1], wot[:, h, m * HALF:(m + 1) * HALF], bias[:, 4, h:h + 1],
                              start=(h == 0), stop=(h == 1))
            last.then_inc(bout_mm, 1)
            pe.wait_ge(w_cast, 1)

            def stay_warm(n, bank=7):
                for _ in range(n):
                    mm(P[:, bank, :], identb[:], junk[:], start=True, stop=True)

            def group_norm(g):
                stay_warm(6)
                pe.wait_ge(g_agg, ONE + 3 * (g + 1))
                mm(P[0:HALF, 6, 0:2], gmat[:], mv[:, :, 0], start=True, stop=True).then_inc(g_mean, 1)
                stay_warm(3)
                pe.wait_ge(g_sq, ONE + g + 1)
                mm(P[0:HALF, 6, 2:4], gmat[:], gsq[:], start=True, stop=True).then_inc(g_var, 1)
                stay_warm(16)

            with pe.Fori(0, B) as i:
                for c in range(CHUNKS):
                    slot = c % 2
                    pe.wait_ge(x_in[slot], ONE + 16 * ((4 - slot) * i + c // 2 + 1))
                    for h in range(2):
                        if c > 0:
                            pe.wait_ge(x_kept, ONE + 2 * (CHUNKS * i + c - 1) + h + 1)
                        for t in range(NT):
                            last = turn(P[0:HALF, h, t * TT:(t + 1) * TT],
                                        xin[:, slot, t, h * HALF:(h + 1) * HALF], ident[0:TT, 0:TT])
                        last.then_inc(x_turned, 1)
                group_norm(2 * i)

                def logits(G, h):
                    if h == 0:
                        pe.wait_ge(xn_ok, ONE + 2 * G + 2)
                        pe.wait_ge(l_kept, ONE + G)
                    last = mm(P[0:LOGITS, 2, 0:CT], wa_s[:, h, :], xn[:, h, :], start=(h == 0), stop=(h == 1))
                    if h == 1:
                        last.then_inc(l_mm, 1)

                def values(G, m, h):
                    last = mm(P[0:HALF, m, 0:CT], wv_s[:, h, m * HALF:(m + 1) * HALF], xn[:, h, :],
                              start=(h == 0), stop=(h == 1))
                    if h == 1:
                        last.then_inc(v_mm, 1)

                def turn_logits(G):
                    pe.wait_ge(l_kept, ONE + G + 1)
                    pe.wait_ge(s_sub, ONE + G)
                    for t in range(NT):
                        last = turn(P[0:TT, 3, t * LP:(t + 1) * LP], lg[:, t * TT:(t + 1) * TT],
                                    ident[0:LP, 0:LP])
                    last.then_inc(l_turned, 1)

                def turn_weights(G):
                    pe.wait_ge(sp_low, ONE + G + 1)
                    pe.wait_ge(a_kept, ONE + G)
                    bank = P[0:HK * SPLITS, 4, :].bitcast(BF16)
                    for h in range(2):
                        for t in range(NT):
                            last = turn(bank[:, h * CT + t * TT:h * CT + (t + 1) * TT],
                                        asp[:, 2 * t + h, :, :].rearrange("p s k -> p (s k)"),
                                        identb[0:TT, 0:TT])
                    last.then_inc(a_turned, 1)

                def project(G, c, m, part):
                    if m == 0 and part == 0:
                        pe.wait_ge(padd_ok, ONE + 2 * PADD * (G + 1))
                    if part < 2:
                        mm(P[0:HALF, m, 0:CT], wp_s[:, part, m * HALF:(m + 1) * HALF], y0[:, part, :],
                           start=(part == 0), stop=False)
                    else:
                        mm(P[0:HALF, m, 0:CT], ident[0:HALF, 0:HALF], xa[:, m, bass.ds(c * ROWS, ROWS), 0:W],
                           start=False, stop=True).then_inc(o_mm, 1)

                def outlook(c, first, last_chunk):
                    G = CHUNKS * i + c
                    side = []

                    def prepare_next():
                        return [lambda: (logits(G + 1, 0), logits(G + 1, 1)),
                                lambda: (pe.wait_ge(x1_kept, ONE + (2 * G if first else 2 * G - 2)),
                                         values(G + 1, 0, 0)),
                                lambda: turn_logits(G + 1), lambda: values(G + 1, 0, 1),
                                lambda: values(G + 1, 1, 0), lambda: values(G + 1, 1, 1)]
                    if not last_chunk:
                        side += prepare_next()
                    if not first:
                        for m in range(2):
                            for part in range(3):
                                def step(m=m, part=part):
                                    if part == 0:
                                        if not last_chunk:
                                            pe.wait_ge(v_kept, ONE + 2 * (G + 1) + m + 1)
                                    project(G - 1, c - 1, m, part)
                                slot = PROJECT_SLOTS[3 * m + part]
                                side += [None] * (slot - len(side)) + [step]
                    side += [None] * (REPS - len(side))
                    if not last_chunk:
                        side[13] = lambda: turn_weights(G + 1)
                    filler = range(6 if first or last_chunk else 15, REPS)
                    if not first:
                        pe.wait_ge(prod_ok, ONE + REPS * G - 2)
                        stay_warm(5, 5)
                    pe.wait_ge(a_kept, ONE + G + 1)
                    par = (c % 2) * 2 * CT
                    for h in range(2):
                        src = at[:, bass.ds(par + h * CT, CT)]
                        for k in range(KK):
                            n = h * KK + k
                            if n >= 3:
                                pe.wait_ge(prod_ok, ONE + REPS * G + n - 2)
                            elif first:
                                pe.wait_ge(prod_ok, ONE + REPS * G)
                            else:
                                pe.wait_ge(prod_ok, ONE + REPS * G + n - 2)
                            if n in filler:
                                stay_warm(1, 5 + n % 3)
                            mm(P[0:HALF, 5 + n % 3, 0:CT], sel[:, k, :], src, start=True, stop=True
                               ).then_inc(rep_mm, 1)
                            if side[n]:
                                side[n]()

                G0 = CHUNKS * i
                logits(G0, 0)
                logits(G0, 1)
                values(G0, 0, 0)
                turn_logits(G0)
                values(G0, 0, 1)
                values(G0, 1, 0)
                values(G0, 1, 1)
                stay_warm(28)
                turn_weights(G0)
                stay_warm(10)
                pe.wait_ge(v_kept, ONE + 2 * G0 + 2)
                outlook(0, True, False)
                with pe.Fori(1, CHUNKS - 1) as c:
                    outlook(c, False, False)
                outlook(CHUNKS - 1, False, True)
                pe.wait_ge(x1_kept, ONE + 2 * (G0 + CHUNKS - 1))
                for m in range(2):
                    for part in range(3):
                        project(G0 + CHUNKS - 1, CHUNKS - 1, m, part)
                group_norm(2 * i + 1)

                def qkv(w, par, j):
                    R = NW * i + w
                    if j == 0:
                        pe.wait_ge(xw_ok, ONE + 2 * R + 2)
                    if j >= 2:
                        pe.wait_ge(qkv_kept, ONE + QKV * R + j - 1)
                    elif not (isinstance(w, int) and w == 0):
                        pe.wait_ge(qkv_kept, ONE + QKV * R + j - 1)
                    for h in range(2):
                        if j < 4:
                            col = C * (1 - j // 2) + (j % 2) * HALF
                            last = mm(P[0:HALF, j % 2, 0:RT], wt[:, h, col:col + HALF], xw[:, par, h, :],
                                      start=(h == 0), stop=(h == 1))
                        else:
                            p = j - 4
                            last = mm(P[0:2 * N, j % 2, 0:C], xw[:, par, h, p * 2 * N:(p + 1) * 2 * N],
                                      wt[:, h, 2 * C:3 * C], start=(h == 0), stop=(h == 1))
                    last.then_inc(qkv_mm, 1)

                def scores(w, par, p):
                    R = NW * i + w
                    Q = PAIRS * R + p
                    if p % 2 == 0:
                        pe.wait_ge(k_in[p // 2], ONE + 16 * BDMA * (R + 1))
                    if p == 0:
                        pe.wait_ge(qkv_kept, ONE + QKV * R + 4)
                    for h in range(2):
                        if not (isinstance(w, int) and w == 0 and p == 0):
                            pe.wait_ge(t_add, ONE + 2 * Q + h - 1)
                        for s in range(2):
                            win = 2 * p + s
                            col = (win * N) % (RT // 2)
                            last = mm(P[s * SLOT:(s + 1) * SLOT, 2 + h, 0:HH * N],
                                      qs[:, par, h, win * N:win * N + SLOT],
                                      kbd[:, p // 2, h, :, col:col + N], start=True, stop=True)
                        last.then_inc(sc_mm, 1)

                def turn_probs(w, p):
                    Q = PAIRS * (NW * i + w) + p
                    pe.wait_ge(p_norm, ONE + Q + 1)
                    for b in range(2):
                        if not (isinstance(w, int) and w == 0 and p == 0):
                            pe.wait_ge(p_kept, ONE + 2 * Q + b - 1)
                        for c in range(3):
                            hp = 3 * b + c
                            last = turn(P[0:2 * N, 4 + b, c * 128:(c + 1) * 128],
                                        ps_[:, p % 2, hp * 2 * N:(hp + 1) * 2 * N], ident[:])
                        last.then_inc(p_turned, 1)

                def attend(w, par, p):
                    R = NW * i + w
                    Q = PAIRS * R + p
                    if p == 0:
                        pe.wait_ge(v_in, ONE + 64 * (R + 1))
                    pe.wait_ge(p_kept, ONE + 2 * Q + 2)
                    pe.wait_ge(y_kept, ONE + Q)
                    for hp in range(NH // 2):
                        for s in range(2):
                            col = (hp // 3) * 2 * N + s * N
                            r0 = 32 * (hp % 3)
                            last = mm(P[r0:r0 + 32, 6, col:col + N],
                                      vbd[:, par, 2 * p + s, 2 * HD * hp:2 * HD * (hp + 1)],
                                      pt[:, p % 2, hp, s, :], start=True, stop=True)
                    last.then_inc(y_mm, 1)

                def project_out(w, par, p):
                    R = NW * i + w
                    n = min(TT, RT - TT * p)
                    if p == 0:
                        pe.wait_ge(y_kept, ONE + PAIRS * (R + 1))
                        pe.wait_ge(xr_ok, ONE + 2 * (R + 1))
                    pe.wait_ge(out_ok, ONE + PAIRS * R + p)
                    for h in range(2):
                        last = mm(P[0:n, 7, 0:C], yt[:, par, h, p * TT:p * TT + n], wot[:, h, :],
                                  start=(h == 0), stop=(h == 1))
                    for h in range(2):
                        last = turn(P[0:n, 7, C + h * HALF:C + (h + 1) * HALF], xr[:, par, h, p * TT:p * TT + n],
                                    ident[0:HALF, 0:HALF])
                    last.then_inc(out_mm, 1)

                def window_row(w, par, first, last_row):
                    for p in range(PAIRS):
                        turn_probs(w, p)
                        if p < 2:
                            scores(w, par, p + 2)
                        elif not last_row:
                            scores(w + 1, 1 - par, p - 2)
                        if not last_row:
                            for j in STEP_TILES[p]:
                                qkv(w + 1, 1 - par, j)
                        attend(w, par, p)
                        if not first:
                            project_out(w - 1, 1 - par, p)

                for j in range(QKV):
                    qkv(0, 0, j)
                scores(0, 0, 0)
                scores(0, 0, 1)
                stay_warm(14)
                window_row(0, 0, True, False)
                with pe.Fori(0, NW // 2 - 1) as u:
                    window_row(2 * u + 1, 1, False, False)
                    window_row(2 * u + 2, 0, False, False)
                window_row(NW - 1, 1, False, True)
                for p in range(PAIRS):
                    project_out(NW - 1, 1, p)

        @block.scalar
        def _(act):
            go = nc.scalar.activation
            for b in range(8):
                act.wait_ge(w_turned, b + 1)
                src = P[0:HALF, b % 4, 0:C].rearrange("p (h n) -> p h n", h=2)
                if b < 2:
                    ins = go(wt[:, :, b * HALF:(b + 1) * HALF], src, ACT.Copy, scale=HD ** -0.5)
                elif b < 6:
                    ins = go(wt[:, :, b * HALF:(b + 1) * HALF], src, ACT.Copy)
                else:
                    ins = go(wot[:, :, (b - 6) * HALF:(b - 5) * HALF], src, ACT.Copy)
                ins.then_inc(w_kept, 1)

            def group_norm(g):
                act.wait_ge(g_table, ONE + 2 * g)
                go(table_t[:], eps_s[:], ACT.Sqrt).then_inc(g_table, 1)
                act.wait_ge(g_var, ONE + g + 1)
                go(gstd[:], P[0:HALF, 6, 2:4], ACT.Sqrt, bias=eps_s[:]).then_inc(g_std, 1)
                act.wait_ge(g_table, ONE + 2 * g + 1)
                go(table_t[:], eps_s[:], ACT.Exp).then_inc(g_table, 1)

            act.wait_ge(zeroed, 9)
            act.wait_ge(wscaled, 1)
            act.wait_ge(bout_ok, 1)
            with act.Fori(0, B) as i:
                for c in range(CHUNKS):
                    for h in range(2):
                        act.wait_ge(x_turned, ONE + 2 * (CHUNKS * i + c) + h + 1)
                        go(xa[:, h, c * ROWS:(c + 1) * ROWS, 0:W],
                           P[0:HALF, h, 0:CT].rearrange("p (r n) -> p r n", n=W), ACT.Copy).then_inc(x_kept, 1)
                group_norm(2 * i)

                def normalize(G, c):
                    for h in range(2):
                        if h == 0:
                            act.wait_ge(l_mm, ONE + G)
                            act.wait_ge(v_mm, ONE + 2 * G)
                        go(xn[:, h, :].rearrange("p (r n) -> p r n", n=W), xa[:, h, bass.ds(c * ROWS, ROWS), 0:W],
                           ACT.Identity, bias=gb[:, h:h + 1], scale=ga[:, h:h + 1]).then_inc(xn_ok, 1)

                def keep_logits(G):
                    act.wait_ge(l_mm, ONE + G + 1)
                    act.wait_ge(l_turned, ONE + G)
                    go(lg[0:LOGITS, :], P[0:LOGITS, 2, 0:CT], ACT.Identity, bias=ba_s[:]).then_inc(l_kept, 1)

                def keep_values(G, c, m):
                    act.wait_ge(v_mm, ONE + 2 * G + m + 1)
                    go(vpad[:, m, bass.ds(c * ROWS + 1, ROWS), 1:W + 1],
                       P[0:HALF, m, 0:CT].rearrange("p (r n) -> p r n", n=W), ACT.Identity,
                       bias=bias[:, 0, m:m + 1]).then_inc(v_kept, 1)

                def exps(G):
                    act.wait_ge(s_sub, ONE + G + 1)
                    act.wait_ge(s_norm, ONE + G)
                    go(sex[:], ssh[:], ACT.Exp).then_inc(s_exp, 1)

                by_half = lambda ap: ap.rearrange("p (n k) -> p n k", k=HK)

                def split_hi(G):
                    act.wait_ge(s_norm, ONE + G + 1)
                    act.wait_ge(a_turned, ONE + G)
                    go(asp[:, :, 0, :], by_half(sa[:]), ACT.Copy).then_inc(sp_hi, 1)

                def split_mid(G):
                    act.wait_ge(sp_rest, ONE + G + 1)
                    go(asp[:, :, 1, :], by_half(srest[:]), ACT.Copy).then_inc(sp_mid, 1)

                def keep_weights(G, c, clamp):
                    act.wait_ge(a_turned, ONE + G + 1)
                    act.wait_ge(rep_mm, ONE + (REPS * G if clamp else REPS * (G - 1)))
                    go(at[:, bass.ds((c % 2) * 2 * CT, 2 * CT)],
                       P[0:HK * SPLITS, 4, :].bitcast(BF16)[:, 0:2 * CT], ACT.Copy).then_inc(a_kept, 1)

                def keep_x1(G, c):
                    for m in range(2):
                        act.wait_ge(o_mm, ONE + 2 * G + m + 1)
                        go(xa[:, m, bass.ds(c * ROWS, ROWS), 0:W],
                           P[0:HALF, m, 0:CT].rearrange("p (r n) -> p r n", n=W), ACT.Identity,
                           bias=bias[:, 1, m:m + 1]).then_inc(x1_kept, 1)

                def outlook(c, first, last_chunk):
                    G = CHUNKS * i + c
                    if not last_chunk:
                        keep_logits(G + 1)
                        keep_values(G + 1, c + 1, 0)
                        exps(G + 1)
                        keep_values(G + 1, c + 1, 1)
                        split_hi(G + 1)
                        split_mid(G + 1)
                        if not (isinstance(c, int) and c == CHUNKS - 2):
                            normalize(G + 2, c + 2)
                    if not first:
                        keep_x1(G - 1, c - 1)
                    if not last_chunk:
                        keep_weights(G + 1, c + 1, first)

                G0 = CHUNKS * i
                act.wait_ge(g_ready, ONE + 2 * (2 * i + 1))
                normalize(G0, 0)
                keep_logits(G0)
                keep_values(G0, 0, 0)
                keep_values(G0, 0, 1)
                normalize(G0 + 1, 1)
                exps(G0)
                split_hi(G0)
                split_mid(G0)
                keep_weights(G0, 0, True)
                outlook(0, True, False)
                with act.Fori(1, CHUNKS - 2) as c:
                    outlook(c, False, False)
                outlook(CHUNKS - 2, False, False)
                outlook(CHUNKS - 1, False, True)
                keep_x1(G0 + CHUNKS - 1, CHUNKS - 1)
                act.wait_ge(x1_kept, ONE + 2 * CHUNKS * (i + 1))
                for h in range(2):
                    go(xa[:, h, 0:H, W:XP], xa[:, h, 0:H, 0:SHIFT], ACT.Copy).then_inc(x1_wrap, 1)
                act.wait_ge(x1_wrap, ONE + 4 * i + 2)
                for h in range(2):
                    go(xa[:, h, H:XP, :], xa[:, h, 0:SHIFT, :], ACT.Copy).then_inc(x1_wrap, 1)
                group_norm(2 * i + 1)

                def keep_qkv(w, par, j):
                    R = NW * i + w
                    act.wait_ge(qkv_mm, ONE + QKV * R + j + 1)
                    if j == 0:
                        for d in range(2):
                            act.wait_ge(k_in[d], ONE + 16 * BDMA * R)
                    if j == 4:
                        act.wait_ge(v_in, ONE + 64 * R)
                    h = j % 2
                    if j < 2:
                        ins = go(ks[:, h, :], P[0:HALF, h, 0:RT], ACT.Identity, bias=bias[:, 3, h:h + 1])
                    elif j < 4:
                        ins = go(qs[:, par, h, 0:RT], P[0:HALF, h, 0:RT], ACT.Identity, bias=bias[:, 6, h:h + 1])
                    else:
                        dst = vs[:, j - 4, :, :].rearrange("p a (c e d) -> p a c e d", e=2, d=HD)
                        src = P[0:2 * N, h, 0:C].rearrange("p (c e d) -> p c e d", e=2, d=HD)
                        go(dst[:, 0, :, 0, :], src[:, :, 0, :], ACT.Copy)
                        ins = go(dst[:, 1, :, 1, :], src[:, :, 1, :], ACT.Copy)
                    ins.then_inc(qkv_kept, 1)

                def exp_pair(w, p):
                    Q = PAIRS * (NW * i + w) + p
                    act.wait_ge(t_sub, ONE + Q + 1)
                    early = isinstance(w, int) and w == 0 and p < 2
                    act.wait_ge(p_turned, ONE + (2 * Q - 2 * p if early else 2 * Q - 2))
                    go(ps_[:, p % 2, :], ts_[:, p % 2, :], ACT.Exp).then_inc(p_exp, 1)

                def keep_probs(w, p):
                    Q = PAIRS * (NW * i + w) + p
                    for b in range(2):
                        act.wait_ge(p_turned, ONE + 2 * Q + b + 1)
                        if b == 0:
                            early = isinstance(w, int) and w == 0 and p < 2
                            act.wait_ge(y_mm, ONE + (Q - p if early else Q - 1))
                        src = P[0:2 * N, 4 + b, 0:384].rearrange("p (c s n) -> p c s n", c=3, s=2)[:, :, :, 0:N]
                        go(pt[:, p % 2, 3 * b:3 * b + 3, :, :], src, ACT.Copy).then_inc(p_kept, 1)

                def keep_residual(w, p):
                    R = NW * i + w
                    n = min(TT, RT - TT * p)
                    act.wait_ge(out_mm, ONE + PAIRS * R + p + 1)
                    act.wait_ge(out_in[p], ONE + 16 * R)
                    go(ot[0:n, p, :], P[0:n, 7, C:2 * C], ACT.Copy).then_inc(res_kept, 1)

                def window_row(w, par, first, last_row):
                    for p in range(PAIRS):
                        if p < 3:
                            exp_pair(w, p + 1)
                        elif not last_row:
                            exp_pair(w + 1, 0)
                        keep_probs(w, p)
                        if not last_row:
                            for j in STEP_TILES[p]:
                                keep_qkv(w + 1, 1 - par, j)
                        if not first:
                            keep_residual(w - 1, p)

                for j in range(QKV):
                    keep_qkv(0, 0, j)
                exp_pair(0, 0)
                window_row(0, 0, True, False)
                with act.Fori(0, NW // 2 - 1) as u:
                    window_row(2 * u + 1, 1, False, False)
                    window_row(2 * u + 2, 0, False, False)
                window_row(NW - 1, 1, False, True)
                for p in range(PAIRS):
                    keep_residual(NW - 1, p)

        @block.vector
        def _(dve):
            tt, ts, red = nc.vector.tensor_tensor, nc.vector.tensor_scalar, nc.vector.tensor_reduce
            nc.vector.memset(ts_[:, 0, :], 0.0).then_inc(rel_zero, 1)
            dve.wait_ge(consts_in, 16 * NCONST)
            nc.vector.tensor_copy(sel[:].rearrange("p k n -> p (k n)"), self32[:]).then_inc(w_cast, 1)
            ts(bias[:, 6, :], bias[:, 2, :], HD ** -0.5, None, ALU.mult).then_inc(wscaled, 1)
            dve.wait_ge(rel_in, 16 * (1 + 2 * WS))
            for v in range(4):
                tt(relb[:, v, :].rearrange("p (h k) -> p h k", h=NH),
                   rel_raw[:, ::-1, :].rearrange("p k h -> p h k"),
                   mask_s[:, v, :].unsqueeze(1).to_broadcast([128, NH, N]), ALU.add).then_inc(rel_ok, 1)
            dve.wait_ge(bout_mm, 1)
            tt(bout[:], P[0:HALF, 4, 0:2], bias[:, 5, :], ALU.add).then_inc(bout_ok, 1)
            dve.wait_ge(rel_ok, 4)
            dve.wait_ge(bout_ok, 1)

            def group_norm(g, stat, n):
                dve.wait_ge(stat, ONE + n)
                nc.vector.memset(fence[:], 0.0).then_inc(g_agg, 1)
                for h in range(2):
                    nc.vector.bn_aggr(mv[:, h, :], stats[:, h, :, :].rearrange("p c s -> p (c s)")).then_inc(g_agg, 1)
                dve.wait_ge(g_agg, ONE + 3 * (g + 1))
                dve.wait_ge(g_mean, ONE + g + 1)
                tt(gdev[:], mv[:, :, 0], P[0:HALF, 6, 0:2], ALU.subtract).then_inc(g_dev, 1)
                nc.vector.tensor_copy(gmean[:], P[0:HALF, 6, 0:2]).then_inc(g_dev, 1)
                dve.wait_ge(g_dev, ONE + 3 * g + 2)
                tt(gdev[:], gdev[:], gdev[:], ALU.mult).then_inc(g_dev, 1)
                dve.wait_ge(g_dev, ONE + 3 * g + 3)
                tt(gsq[:], gdev[:], mv[:, :, 1], ALU.add).then_inc(g_sq, 1)
                dve.wait_ge(g_std, ONE + g + 1)
                nc.vector.reciprocal(ga[:], gstd[:]).then_inc(g_rstd, 1)
                dve.wait_ge(g_rstd, ONE + g + 1)
                nc.vector.scalar_tensor_tensor(out=gb[:], in0=gmean[:], scalar=-1.0, in1=ga[:],
                                               op0=ALU.mult, op1=ALU.mult).then_inc(g_ready, 2)

            with dve.Fori(0, B) as i:
                for c in range(CHUNKS):
                    for h in range(2):
                        dve.wait_ge(x_kept, ONE + 2 * (CHUNKS * i + c) + h + 1)
                        nc.vector.bn_stats(stats[:, h, c, :], xa[:, h, c * ROWS:(c + 1) * ROWS, 0:W]
                                           ).then_inc(x_stat, 1)
                group_norm(2 * i, x_stat, 2 * CHUNKS * (i + 1))

                by_head = lambda ap: ap.rearrange("p (n k) -> p n k", k=KK)
                by_tile = lambda ap: ap.rearrange("p (t h) -> p t h", t=NT)

                def soft_shift(G):
                    dve.wait_ge(l_turned, ONE + G + 1)
                    logit = P[0:TT, 3, 0:NT * LP].rearrange("p (t l) -> p t l", t=NT)[:, :, 0:LOGITS].rearrange(
                        "p t (h k) -> p t h k", k=KK)
                    red(by_tile(smx[:]), logit, AX.X, ALU.max).then_inc(s_max, 1)
                    dve.wait_ge(s_max, ONE + G + 1)
                    dve.wait_ge(s_exp, ONE + G)
                    tt(ssh[:].rearrange("p (t h k) -> p t h k", t=NT, k=KK), logit,
                       by_tile(smx[:]).unsqueeze(3).to_broadcast([TT, NT, OHEADS, KK]), ALU.subtract).then_inc(s_sub, 1)

                def soft_sum(G):
                    dve.wait_ge(s_exp, ONE + G + 1)
                    red(ssum[:], by_head(sex[:]), AX.X, ALU.add).then_inc(s_sum, 1)
                    dve.wait_ge(s_sum, ONE + G + 1)
                    dve.wait_ge(s_norm, ONE + G)
                    nc.vector.reciprocal(srec[:], ssum[:]).then_inc(s_rec, 1)

                def stat_x1(G, c):
                    for m in range(2):
                        dve.wait_ge(x1_kept, ONE + 2 * G + m + 1)
                        nc.vector.bn_stats(stats[:, m, bass.ds(c, 1), :].rearrange("p a s -> p (a s)"),
                                           xa[:, m, bass.ds(c * ROWS, ROWS), 0:W]).then_inc(x1_stat, 1)

                def outlook(c, first, last_chunk):
                    G = CHUNKS * i + c
                    dve.wait_ge(v_kept, ONE + 2 * (G + 1))
                    for h in range(2):
                        for k in range(KK):
                            n = h * KK + k
                            di, dj = k // 3, k % 3
                            dve.wait_ge(rep_mm, ONE + REPS * G + n + 1)
                            if k < RING:
                                dst = prod[:, k, :]
                                if h == 0 and first:
                                    dve.wait_ge(padd_ok, ONE + 2 * PADD * G)
                                else:
                                    dve.wait_ge(padd_ok, ONE + 2 * PADD * G + PADD * (h - 1) + max(k, 1))
                            else:
                                dst = ptail[:, k - RING, :]
                                if k == RING:
                                    dve.wait_ge(padd_ok, ONE + 2 * PADD * G + PADD * h)
                            if di == 2 and dj == 0 and not last_chunk:
                                dve.wait_ge(v_kept, ONE + 2 * (G + 1) + h + 1)
                            tt(dst.rearrange("p (r n) -> p r n", n=W),
                               P[0:HALF, 5 + n % 3, 0:CT].rearrange("p (r n) -> p r n", n=W),
                               vpad[:, h, bass.ds(c * ROWS + di, ROWS), dj:dj + W], ALU.mult).then_inc(prod_ok, 1)
                            if not last_chunk and n == 3:
                                soft_shift(G + 1)
                            if not last_chunk and n == 6:
                                soft_sum(G + 1)
                        dve.wait_ge(prod_ok, ONE + REPS * G + h * KK + KK)
                        tt(ptail[:, 0, :], ptail[:, 0, :], ptail[:, 1, :], ALU.add).then_inc(tail_ok, 1)
                        dve.wait_ge(tail_ok, ONE + 4 * G + 2 * h + 1)
                        tt(ptail[:, 0, :], ptail[:, 0, :], ptail[:, 2, :], ALU.add).then_inc(tail_ok, 1)
                    if not first:
                        stat_x1(G - 1, c - 1)

                G0 = CHUNKS * i
                soft_shift(G0)
                soft_sum(G0)
                outlook(0, True, False)
                with dve.Fori(1, CHUNKS - 1) as c:
                    outlook(c, False, False)
                outlook(CHUNKS - 1, False, True)
                stat_x1(G0 + CHUNKS - 1, CHUNKS - 1)
                group_norm(2 * i + 1, x1_stat, 2 * CHUNKS * (i + 1))
                dve.wait_ge(x1_wrap, ONE + 4 * (i + 1))
                dve.wait_ge(g_ready, ONE + 2 * (2 * i + 2))

                def stage_norm(w, par, h):
                    R = NW * i + w
                    dve.wait_ge(qkv_mm, ONE + (QKV * NW * i if isinstance(w, int) and w < 2 else QKV * (R - 1)))
                    rows = xa[:, h, bass.ds(WS * w + SHIFT, WS), SHIFT:XP].rearrange("p r (j c) -> p j r c", c=WS)
                    ts(xw[:, par, h, :].rearrange("p (j r c) -> p j r c", r=WS, c=WS), rows,
                       ga[:, h:h + 1], gb[:, h:h + 1], ALU.mult, ALU.add).then_inc(xw_ok, 1)

                def stage_residual(w, par, h):
                    R = NW * i + w
                    dve.wait_ge(out_mm, ONE + (PAIRS * NW * i if isinstance(w, int) and w < 2 else PAIRS * (R - 1)))
                    ts(xr[:, par, h, :].rearrange("p (r n) -> p r n", n=W),
                       xa[:, h, bass.ds(WS * w + SHIFT, WS), 0:W], bout[:, h:h + 1], None,
                       ALU.add).then_inc(xr_ok, 1)

                def score_max(w, p, bottom):
                    Q = PAIRS * (NW * i + w) + p
                    kind = 2 * bottom + (p == PAIRS - 1)
                    early = isinstance(w, int) and w == 0 and p < 2
                    dve.wait_ge(p_exp, ONE + (Q - p if early else Q - 1))
                    for h in range(2):
                        dve.wait_ge(sc_mm, ONE + 2 * Q + h + 1)
                        cols = slice(h * HH * N, (h + 1) * HH * N)
                        tt(ts_[:, p % 2, cols], P[:, 2 + h, 0:HH * N], relb[:, kind, cols], ALU.add).then_inc(t_add, 1)
                    dve.wait_ge(t_add, ONE + 2 * Q + 2)
                    red(mx[:, p % 2, :], ts_[:, p % 2, :].rearrange("p (h k) -> p h k", h=NH), AX.X,
                        ALU.max).then_inc(t_max, 1)

                def prob_sum(w, p):
                    Q = PAIRS * (NW * i + w) + p
                    early = isinstance(w, int) and w == 0 and p < 2
                    dve.wait_ge(p_norm, ONE + (Q - p if early else Q - 1))
                    dve.wait_ge(p_exp, ONE + Q + 1)
                    red(sm[:, p % 2, :], ps_[:, p % 2, :].rearrange("p (h k) -> p h k", h=NH), AX.X,
                        ALU.add).then_inc(p_sum, 1)
                    dve.wait_ge(p_sum, ONE + Q + 1)
                    nc.vector.reciprocal(rc[:, p % 2, :], sm[:, p % 2, :]).then_inc(p_rec, 1)

                def keep_y(w, par, p):
                    R = NW * i + w
                    Q = PAIRS * R + p
                    dve.wait_ge(y_mm, ONE + Q + 1)
                    if p == 0:
                        dve.wait_ge(out_mm, ONE + (PAIRS * NW * i if isinstance(w, int) and w < 2 else PAIRS * (R - 1)))
                    for h in range(2):
                        src = P[0:HALF, 6, h * 2 * N:(h + 1) * 2 * N].rearrange("p (s r c) -> p s r c", s=2, c=WS)
                        dst = yt[:, par, h, :].rearrange("p (r n) -> p r n", n=W)
                        col = SHIFT + 2 * WS * p
                        if p < PAIRS - 1:
                            last = nc.vector.tensor_copy(
                                dst[:, :, col:col + 2 * WS].rearrange("p r (s c) -> p s r c", s=2), src)
                        else:
                            nc.vector.tensor_copy(dst[:, :, col:col + WS], src[:, 0, :, :])
                            nc.vector.tensor_copy(dst[:, :, col + WS:W], src[:, 1, :, 0:WS - SHIFT])
                            last = nc.vector.tensor_copy(dst[:, :, 0:SHIFT], src[:, 1, :, WS - SHIFT:WS])
                    last.then_inc(y_kept, 1)

                def finish(w, p):
                    R = NW * i + w
                    n = min(TT, RT - TT * p)
                    dve.wait_ge(res_kept, ONE + PAIRS * R + p + 1)
                    tt(ot[0:n, p, :], ot[0:n, p, :], P[0:n, 7, 0:C], ALU.add).then_inc(out_ok, 1)

                def window_row(w, par, first, last_row):
                    bottom = last_row
                    for p in range(PAIRS):
                        if p < 3:
                            prob_sum(w, p + 1)
                        elif not last_row:
                            prob_sum(w + 1, 0)
                        if p < 2:
                            score_max(w, p + 2, bottom)
                        elif not last_row:
                            score_max(w + 1, p - 2, w == NW - 2 if isinstance(w, int) else False)
                        keep_y(w, par, p)
                        if not first:
                            finish(w - 1, p)
                        if p >= 2:
                            stage_residual(w, par, p - 2)
                        elif not last_row and not (isinstance(w, int) and w == NW - 2):
                            stage_norm(w + 2, par, p)

                for w in range(2):
                    for h in range(2):
                        stage_norm(w, w, h)
                score_max(0, 0, False)
                score_max(0, 1, False)
                prob_sum(0, 0)
                window_row(0, 0, True, False)
                with dve.Fori(0, NW // 2 - 2) as u:
                    window_row(2 * u + 1, 1, False, False)
                    window_row(2 * u + 2, 0, False, False)
                window_row(NW - 3, 1, False, False)
                window_row(NW - 2, 0, False, False)
                window_row(NW - 1, 1, False, True)
                for p in range(PAIRS):
                    finish(NW - 1, p)

        @block.gpsimd
        def _(pool):
            pool.memset(ident[:], 0.0).then_inc(idents, 1)
            pool.wait_ge(idents, 1)
            pool.affine_select(out=ident[:], in_=ident[:], compare_op=ALU.not_equal, fill=1.0, base=0,
                               pattern=[[-1, 128]], channel_multiplier=1).then_inc(idents, 1)
            pool.wait_ge(idents, 2)
            pool.tensor_copy(identb[:], ident[:]).then_inc(idents, 1)
            for s in counted:
                pool.sem_inc(s, ONE)
            pool.memset(kbd[:], 0.0).then_inc(zeroed, 1)
            pool.memset(vbd[:], 0.0).then_inc(zeroed, 1)
            pool.memset(lg[:], 0.0).then_inc(zeroed, 1)
            pool.memset(vs[:], 0.0).then_inc(zeroed, 1)
            pool.memset(vpad[:, 0, :, :], 0.0).then_inc(zeroed, 1)
            pool.memset(vpad[:, 1, :, :], 0.0).then_inc(zeroed, 1)
            pool.memset(qs[:, 0, :, :], 0.0).then_inc(zeroed, 1)
            pool.memset(qs[:, 1, :, :], 0.0).then_inc(zeroed, 1)
            pool.memset(junk[:], 0.0).then_inc(idents, 1)
            pool.memset(eps_s[:], EPS).then_inc(zeroed, 1)
            tt = nc.gpsimd.tensor_tensor
            by_head = lambda ap: ap.rearrange("p (n k) -> p n k", k=KK)
            by_half = lambda ap: ap.rearrange("p (n k) -> p n k", k=HK)

            with pool.Fori(0, B) as i:
                def soft_split(G, step):
                    if step == 0:
                        pool.wait_ge(sp_low, ONE + G)
                        pool.wait_ge(s_rec, ONE + G + 1)
                        tt(by_head(sa[:]), by_head(sex[:]),
                           srec[:].unsqueeze(2).to_broadcast([TT, NT * OHEADS, KK]), ALU.mult).then_inc(s_norm, 1)
                    elif step == 1:
                        pool.wait_ge(sp_hi, ONE + G + 1)
                        tt(by_half(srest[:]), by_half(sa[:]), asp[:, :, 0, :], ALU.subtract).then_inc(sp_rest, 1)
                    else:
                        pool.wait_ge(sp_mid, ONE + G + 1)
                        tt(asp[:, :, 2, :], by_half(srest[:]), asp[:, :, 1, :], ALU.subtract).then_inc(sp_low, 1)

                def outlook(c, last_chunk):
                    G = CHUNKS * i + c
                    for h in range(2):
                        A = 2 * PADD * G + PADD * h
                        D = REPS * G + KK * h
                        pool.wait_ge(padd_ok, ONE + A)
                        pool.wait_ge(prod_ok, ONE + D + 2)
                        tt(psum_p[:], prod[:, 0, :], prod[:, 1, :], ALU.add).then_inc(padd_ok, 1)
                        for k in range(2, RING):
                            pool.wait_ge(prod_ok, ONE + D + k + 1)
                            pool.wait_ge(padd_ok, ONE + A + k - 1)
                            tt(psum_p[:], psum_p[:], prod[:, k, :], ALU.add).then_inc(padd_ok, 1)
                            if h == 0 and k >= RING - 3 and not last_chunk:
                                soft_split(G + 1, k - (RING - 3))
                        pool.wait_ge(tail_ok, ONE + 4 * G + 2 * h + 2)
                        pool.wait_ge(padd_ok, ONE + A + PADD - 1)
                        pool.wait_ge(o_mm, ONE + 2 * G)
                        tt(y0[:, h, :], psum_p[:], ptail[:, 0, :], ALU.add).then_inc(padd_ok, 1)

                G0 = CHUNKS * i
                for step in range(3):
                    soft_split(G0, step)
                outlook(0, False)
                with pool.Fori(1, CHUNKS - 1) as c:
                    outlook(c, False)
                outlook(CHUNKS - 1, True)

                per_head = lambda ap: ap.rearrange("p (h k) -> p h k", h=NH)
                spread = lambda ap: ap.unsqueeze(2).to_broadcast([128, NH, N])

                def shift_pair(w, p):
                    Q = PAIRS * (NW * i + w) + p
                    pool.wait_ge(t_max, ONE + Q + 1)
                    tt(per_head(ts_[:, p % 2, :]), per_head(ts_[:, p % 2, :]), spread(mx[:, p % 2, :]),
                       ALU.subtract).then_inc(t_sub, 1)

                def normalize_pair(w, p):
                    Q = PAIRS * (NW * i + w) + p
                    pool.wait_ge(p_rec, ONE + Q + 1)
                    tt(per_head(ps_[:, p % 2, :]), per_head(ps_[:, p % 2, :]), spread(rc[:, p % 2, :]),
                       ALU.mult).then_inc(p_norm, 1)

                def window_row(w, last_row):
                    for p in range(PAIRS):
                        if p < 3:
                            normalize_pair(w, p + 1)
                        elif not last_row:
                            normalize_pair(w + 1, 0)
                        if p < 2:
                            shift_pair(w, p + 2)
                        elif not last_row:
                            shift_pair(w + 1, p - 2)

                shift_pair(0, 0)
                shift_pair(0, 1)
                normalize_pair(0, 0)
                with pool.Fori(0, NW - 1) as w:
                    window_row(w, False)
                window_row(NW - 1, True)


_INS = ["x", "L0_conv_W_attn", "L0_conv_b_attn", "L0_conv_W_v", "L0_conv_b_v", "L0_conv_W_proj",
        "L0_conv_b_proj", "L1_conv_qkv_weight", "L1_conv_qkv_bias", "L1_conv_proj_weight",
        "L1_conv_proj_bias", "L1_conv_rel_pos_bias_table"]


def _constants():
    sel = np.zeros((SPLITS, 3, KK, KK, 3, C // OHEADS), np.float32)
    for h in range(3):
        for k in range(KK):
            sel[:, h, k, k, h, :] = 1.0
    sel = sel.reshape(SPLITS * HK, KK * HALF)
    gmat = np.kron(np.eye(HALF // GROUP), np.full((GROUP, GROUP), 1.0 / GROUP)).astype(np.float32)
    mask = np.zeros((128, 4, N), np.float32)
    pos = np.arange(N)
    for bottom in range(2):
        for right in range(2):
            for s in range(2):
                region = np.zeros(N, np.int64)
                if bottom:
                    region += 2 * (pos // WS >= WS - SHIFT)
                if right and s:
                    region += pos % WS >= WS - SHIFT
                mask[s * SLOT:s * SLOT + N, 2 * bottom + right, :] = np.where(
                    region[:, None] != region[None, :], -100.0, 0.0)
    return {"sel": sel, "gmat": gmat, "mask": mask}


def kernel(**inputs):
    import concourse.bacc as _bacc
    from concourse.bass_utils import run_bass_kernel_spmd as _run

    nc = _bacc.Bacc("TRN2", target_bir_lowering=False, num_devices=1)
    arrays, args = {}, []
    for name in _INS:
        a = np.ascontiguousarray(inputs[name])
        if name == "x":
            a = a.reshape(B * H * W, C)
        arrays[f"in_{name}"] = a
        args.append(nc.dram_tensor(f"in_{name}", a.shape, mybir.dt.from_np(a.dtype), kind="ExternalInput").ap())
    for name, a in _constants().items():
        arrays[f"in_{name}"] = a
        args.append(nc.dram_tensor(f"in_{name}", a.shape, mybir.dt.from_np(a.dtype), kind="ExternalInput").ap())
    args.append(nc.dram_tensor("out", (B * H * W, C), F32, kind="ExternalOutput").ap())
    mixer(nc, *args)
    r = _run(nc, [arrays], core_ids=[0])
    return np.asarray(r.results[0]["out"]).reshape(B, H, W, C)
```

```python
from contextlib import ExitStack

import numpy as np

import concourse.bass as bass
from concourse import mybir

F32 = mybir.dt.float32
BF16 = mybir.dt.bfloat16
ALU = mybir.AluOpType
ACT = mybir.ActivationFunctionType
AX = mybir.AxisListType

B, H, W, C = 16, 56, 56, 192
HALF = C // 2
EPS = 1e-5
GROUP = C // 32
OHEADS, KK = 6, 9
LOGITS = OHEADS * KK
LP = 66
HK = LOGITS // 2
SPLITS = 3
ROWS = 8
CHUNKS = H // ROWS
CT = ROWS * W
TT = 112
NT = CT // TT
REPS = 2 * KK
PROJECT_SLOTS = (6, 7, 8, 9, 10, 11)
RING = 6
PADD = 6
OWN = (6, 6)
OWN_LAST = (5, 4)
TAILS = 2 * (KK - 1) - sum(OWN)
TAILS_LAST = 2 * (KK - 1) - sum(OWN_LAST)
WS, SHIFT = 7, 3
NH, HD = 12, 16
NW = W // WS
N = WS * WS
RT = NW * N
PAIRS = NW // 2
SLOT = 64
HH = NH // 2
NTAB = 2 * WS - 1
XP = W + SHIFT
ONE = 1
QKV = 8
STEP_TILES = ((0, 1), (2, 3, 4), (5, 6, 7), ())
G1_BANK, G2_BANK = 0, 6
TURN_LAST = 0
BDMA = HH


def mixer(nc, x, wa, ba, wv, bv, wp, bp, wqkv, bqkv, wo, bo, table, sel_in, gmat_in, mask_in, out):
    ctx = ExitStack()
    with ctx:
        def sb(name, shape, dt=F32):
            return ctx.enter_context(nc.sbuf_tensor(name, shape, dt))

        def sem(name):
            return ctx.enter_context(nc.semaphore(name))

        ident = sb("ident", [128, 128])
        identb = sb("identb", [128, 128], BF16)
        gmat = sb("gmat", [HALF, HALF])
        self32 = sb("self32", [HK * SPLITS, KK * HALF])
        sel = sb("sel", [HK * SPLITS, KK, HALF], BF16)
        wa_s = sb("wa_s", [HALF, 2, LOGITS])
        ba_s = sb("ba_s", [LOGITS, 1])
        wv_s = sb("wv_s", [HALF, 2, C])
        wp_s = sb("wp_s", [HALF, 2, C])
        bias = sb("bias", [HALF, 7, 2])
        bout = sb("bout", [HALF, 2])
        wt = sb("wt", [HALF, 2, 3 * C])
        wot = sb("wot", [HALF, 2, C])
        eps_s = sb("eps_s", [HALF, 1])
        relb = sb("relb", [128, 4, NH * N])
        junk = sb("junk", [128, 512], BF16)
        xin = sb("xin", [TT, 2, NT, C])
        xa = sb("xa", [HALF, 2, XP, XP])
        vpad = sb("vpad", [HALF, 2, H + 2, W + 2])
        stats = sb("stats", [HALF, 2, CHUNKS, 6])
        fence = sb("fence", [HALF, 1])
        table_t = sb("table_t", [HALF, 1])
        mv = sb("mv", [HALF, 2, 2])
        gdev = sb("gdev", [HALF, 2])
        gmean = sb("gmean", [HALF, 2])
        gsq = sb("gsq", [HALF, 2])
        gstd = sb("gstd", [HALF, 2])
        ga = sb("ga", [HALF, 2])
        gb = sb("gb", [HALF, 2])
        xn = sb("xn", [HALF, 2, CT])
        lg = sb("lg", [LP, CT])
        smx = sb("smx", [TT, NT * OHEADS])
        ssh = sb("ssh", [TT, NT * LOGITS])
        sex = sb("sex", [TT, NT * LOGITS])
        ssum = sb("ssum", [TT, NT * OHEADS])
        srec = sb("srec", [TT, NT * OHEADS])
        sa = sb("sa", [TT, NT * LOGITS])
        srest = sb("srest", [TT, NT * LOGITS])
        asp = sb("asp", [TT, NT * 2, SPLITS, HK], BF16)
        at = sb("at", [HK * SPLITS, 2 * 2 * CT], BF16)
        prod = sb("prod", [HALF, RING, CT])
        ptail = sb("ptail", [HALF, 2, 3, CT])
        psum_p = sb("psum_p", [HALF, CT])
        y0 = sb("y0", [HALF, 2, CT])
        xw = sb("xw", [HALF, 2, 2, RT])
        xr = sb("xr", [HALF, 2, 2, RT])
        qs = sb("qs", [HALF, 2, 2, RT + SLOT - N])
        ks = sb("ks", [HALF, 2, RT])
        kbd = sb("kbd", [HALF, 2, 2, HH, RT // 2])
        vs = sb("vs", [2 * N, PAIRS, 2, C])
        vbd = sb("vbd", [2 * N, 2, NW, C])
        ts_ = sb("ts_", [128, 2, NH * N])
        ps_ = sb("ps_", [128, 2, NH * N])
        mx = sb("mx", [128, 2, NH])
        sm = sb("sm", [128, 2, NH])
        rc = sb("rc", [128, 2, NH])
        pt = sb("pt", [2 * N, 2, NH // 2, 2, N])
        yt = sb("yt", [HALF, 2, 2, RT])
        ot = sb("ot", [TT, PAIRS, C])
        P = ctx.enter_context(nc.psum_tensor("P", [128, 8, 512], F32))
        wn = prod[:, :, :].rearrange("p a b -> p (a b)")[:, 0:6 * C].rearrange("p (a b) -> p a b", a=6)
        wno = ptail[:, 0, 0, 0:2 * C].rearrange("p (a b) -> p a b", a=2)
        rel_raw = ts_[:, 0, :].rearrange("p (k h) -> p k h", h=NH)
        mask_s = ps_[:, 0, 0:4 * N].rearrange("p (v k) -> p v k", v=4)

        consts_in = sem("consts_in"); rel_in = sem("rel_in")
        zeroed = sem("zeroed"); rel_zero = sem("rel_zero"); idents = sem("idents"); w_cast = sem("w_cast")
        w_turned = sem("w_turned"); w_kept = sem("w_kept"); bout_mm = sem("bout_mm"); bout_ok = sem("bout_ok")
        rel_ok = sem("rel_ok"); wscaled = sem("wscaled")
        x_in = [sem("x_in0"), sem("x_in1")]
        x_turned = sem("x_turned"); x_kept = sem("x_kept"); x_stat = sem("x_stat")
        g_agg = sem("g_agg"); g_table = sem("g_table"); g_mean = sem("g_mean"); g_dev = sem("g_dev"); g_sq = sem("g_sq")
        g_var = sem("g_var"); g_std = sem("g_std"); g_rstd = sem("g_rstd"); g_ready = sem("g_ready")
        xn_ok = sem("xn_ok"); l_mm = sem("l_mm"); l_kept = sem("l_kept"); l_turned = sem("l_turned")
        v_mm = sem("v_mm"); v_kept = sem("v_kept")
        s_max = sem("s_max"); s_sub = sem("s_sub"); s_exp = sem("s_exp"); s_sum = sem("s_sum")
        s_rec = sem("s_rec"); s_norm = sem("s_norm"); sp_hi = sem("sp_hi"); sp_rest = sem("sp_rest")
        sp_mid = sem("sp_mid"); sp_low = sem("sp_low"); a_turned = sem("a_turned"); a_kept = sem("a_kept")
        rep_mm = sem("rep_mm"); prod_ok = sem("prod_ok"); tail_ok = sem("tail_ok"); padd_ok = sem("padd_ok")
        o_mm = sem("o_mm"); x1_kept = sem("x1_kept"); x1_stat = sem("x1_stat"); x1_wrap = sem("x1_wrap")
        xw_ok = sem("xw_ok"); xr_ok = sem("xr_ok"); qkv_mm = sem("qkv_mm"); qkv_kept = sem("qkv_kept")
        k_in = [sem("k_in0"), sem("k_in1")]; v_in = sem("v_in")
        sc_mm = sem("sc_mm"); t_add = sem("t_add"); t_max = sem("t_max"); t_sub = sem("t_sub")
        p_exp = sem("p_exp"); p_sum = sem("p_sum"); p_rec = sem("p_rec"); p_norm = sem("p_norm")
        p_turned = sem("p_turned"); p_kept = sem("p_kept"); y_mm = sem("y_mm"); y_kept = sem("y_kept")
        out_mm = sem("out_mm"); res_kept = sem("res_kept"); out_ok = sem("out_ok")
        out_in = [sem(f"out_in{p}") for p in range(PAIRS)]

        counted = [x_turned, g_table, x_kept, x_stat, g_agg, g_mean, g_dev, g_sq, g_var, g_std,
                   g_rstd, g_ready, xn_ok, l_mm, l_kept, l_turned, v_mm, v_kept, s_max,
                   s_sub, s_exp, s_sum, s_rec, s_norm, sp_hi, sp_rest, sp_mid, sp_low,
                   a_turned, a_kept, rep_mm, prod_ok, tail_ok, padd_ok, o_mm, x1_kept, x1_stat,
                   x1_wrap, xw_ok, xr_ok, qkv_mm, qkv_kept, v_in, sc_mm, t_add, t_max,
                   t_sub, p_exp, p_sum, p_rec, p_norm, p_turned, p_kept, y_mm, y_kept,
                   out_mm, res_kept, out_ok, *x_in, *k_in, *out_in]

        block = ctx.enter_context(nc.Block())

        def x_load(sp, i, c, slot):
            src = x[bass.ds(i * (H * W) + c * CT, CT), :].rearrange("(t p) n -> p t n", p=TT)
            return sp.dma_start(xin[:, slot, :, :], src)

        NCONST = 20

        def tails(i, G):
            return TAILS * G + (TAILS_LAST - TAILS) * i

        @block.sync
        def _(sp):
            def load_bias(j, v):
                for h in range(2):
                    sp.dma_start(bias[:, j, h:h + 1], v[h * HALF:(h + 1) * HALF].rearrange("(p a) -> p a", a=1)
                                 ).then_inc(consts_in, 16)

            sp.dma_start(wn, wqkv.rearrange("(b p) n -> p b n", p=HALF)).then_inc(consts_in, 16)
            sp.dma_start(wno, wo.rearrange("(b p) n -> p b n", p=HALF)).then_inc(consts_in, 16)
            sp.dma_start(wa_s[:], wa.rearrange("(h p) n -> p h n", p=HALF)).then_inc(consts_in, 16)
            sp.dma_start(wv_s[:], wv.rearrange("(h p) n -> p h n", p=HALF)).then_inc(consts_in, 16)
            sp.dma_start(wp_s[:], wp.rearrange("(h p) n -> p h n", p=HALF)).then_inc(consts_in, 16)
            sp.dma_start(gmat[:], gmat_in).then_inc(consts_in, 16)
            sp.dma_start(self32[:], sel_in).then_inc(consts_in, 16)
            sp.dma_start(ba_s[:], ba.rearrange("(p a) -> p a", a=1)).then_inc(consts_in, 16)
            load_bias(0, bv)
            load_bias(1, bp)
            for j in range(3):
                load_bias(2 + j, bqkv[j * C:(j + 1) * C])
            load_bias(5, bo)
            sp.dma_start(mask_s, mask_in).then_inc(rel_in, 16)
            sp.wait_ge(rel_zero, 1)
            for s in range(2):
                for r in range(WS):
                    p0 = s * SLOT + r * WS
                    src = bass.AP(tensor=table.tensor, offset=table.offset + r * NTAB * NH,
                                  ap=[[NH, WS], [NTAB * NH, WS], [1, WS * NH]])
                    dst = ts_[p0:p0 + WS, 0, :].rearrange("p (a b) -> p a b", a=WS)
                    sp.dma_start(dst, src).then_inc(rel_in, 16)
            for c in range(CHUNKS):
                if c >= 2:
                    sp.wait_ge(x_turned, ONE + 2 * (c - 1))
                x_load(sp, 0, c, c % 2).then_inc(x_in[c % 2], 16)

            with sp.Fori(0, B) as i:
                after = sp.snap((i + 1) % B)
                sp.wait_ge(x_turned, ONE + 2 * CHUNKS * (i + 1))
                for c in range(2):
                    x_load(sp, after, c, c).then_inc(x_in[c], 16)

                def spread_k(w, d):
                    R = NW * i + w
                    made = sp.to_reg(ONE + QKV * R + 2)
                    used = sp.to_reg(ONE + 2 * PAIRS * R
                                     + (0 if isinstance(w, int) and w == 0 else 4 * d + 4 - 2 * PAIRS))
                    sp.wait_ge(qkv_kept, made)
                    sp.wait_ge(sc_mm, used)
                    for m in range(HH):
                        sp.dma_start(kbd[HD * m:HD * m + HD, d, :, m, :],
                                     ks[HD * m:HD * m + HD, :, d * (RT // 2):(d + 1) * (RT // 2)]
                                     ).then_inc(k_in[d], 16)

                def spread_v(w, par):
                    R = NW * i + w
                    made = sp.to_reg(ONE + QKV * (R + 1))
                    used = sp.to_reg(ONE + (PAIRS * NW * i if isinstance(w, int) and w < 2 else PAIRS * (R - 1)))
                    sp.wait_ge(qkv_kept, made)
                    sp.wait_ge(y_mm, used)
                    for s in range(2):
                        for e in range(2):
                            sp.dma_start(vbd[N * e:N * e + N, par, s::2, :],
                                         vs[N * s:N * s + N, :, e, :]).then_inc(v_in, 16)

                def store(w, p):
                    R = NW * i + w
                    sp.wait_ge(out_ok, ONE + PAIRS * R + p + 1)
                    row = WS * w + SHIFT + 2 * p
                    if isinstance(w, int):
                        row %= H
                    n = min(TT, RT - TT * p)
                    sp.dma_start(out[bass.ds(i * (H * W) + row * W, n), :], ot[0:n, p, :]
                                 ).then_inc(out_in[p], 16)

                def row_dmas(w, par, first, last, loads):
                    if not last:
                        spread_k(w + 1, 0)
                    if not first:
                        store(w - 1, 0)
                    if not last:
                        spread_k(w + 1, 1)
                    if not first:
                        store(w - 1, 1)
                    if not last:
                        spread_v(w + 1, 1 - par)
                    if not first:
                        store(w - 1, 2)
                    if loads:
                        sp.wait_ge(x_turned, ONE + 2 * (CHUNKS * (i + 1) + w))
                        x_load(sp, after, w + 1, 1 - par).then_inc(x_in[1 - par], 16)
                    if not first:
                        store(w - 1, 3)

                spread_k(0, 0)
                spread_k(0, 1)
                spread_v(0, 0)
                row_dmas(0, 0, True, False, False)
                with sp.Fori(0, NW // 2 - 2) as u:
                    row_dmas(2 * u + 1, 1, False, False, True)
                    row_dmas(2 * u + 2, 0, False, False, True)
                row_dmas(NW - 3, 1, False, False, True)
                row_dmas(NW - 2, 0, False, False, False)
                row_dmas(NW - 1, 1, False, True, False)
                for p in range(PAIRS):
                    store(NW - 1, p)
            for p in range(PAIRS):
                sp.wait_ge(out_in[p], ONE + 16 * B * NW)
            for slot in range(2):
                sp.wait_ge(x_in[slot], ONE + 16 * (4 - slot) * (B + 1))

        @block.tensor
        def _(pe):
            mm, turn = nc.tensor.matmul, nc.tensor.transpose
            pe.wait_ge(idents, 4)
            pe.wait_ge(consts_in, 16 * NCONST)
            for b in range(8):
                src = wn[:, b, :] if b < 6 else wno[:, b - 6, :]
                if b >= 4:
                    pe.wait_ge(w_kept, b - 3)
                for h in range(2):
                    last = turn(P[0:HALF, b % 4, h * HALF:(h + 1) * HALF], src[:, h * HALF:(h + 1) * HALF],
                                ident[0:HALF, 0:HALF])
                last.then_inc(w_turned, 1)
            pe.wait_ge(w_kept, 8)
            for m in range(2):
                for h in range(2):
                    last = mm(P[0:HALF, 4, m:m + 1], wot[:, h, m * HALF:(m + 1) * HALF], bias[:, 4, h:h + 1],
                              start=(h == 0), stop=(h == 1))
            last.then_inc(bout_mm, 1)
            pe.wait_ge(w_cast, 1)

            def stay_warm(n, bank=7):
                for _ in range(n):
                    mm(P[:, bank, :], identb[:], junk[:], start=True, stop=True)

            def group_means(g, bank):
                pe.wait_ge(g_agg, ONE + 3 * (g + 1))
                mm(P[0:HALF, bank, 0:2], gmat[:], mv[:, :, 0], start=True, stop=True).then_inc(g_mean, 1)

            def group_variances(g, bank):
                pe.wait_ge(g_sq, ONE + g + 1)
                mm(P[0:HALF, bank, 2:4], gmat[:], gsq[:], start=True, stop=True).then_inc(g_var, 1)

            def turn_x(h, slot):
                for t in range(NT):
                    last = turn(P[0:HALF, h, t * TT:(t + 1) * TT],
                                xin[:, slot, t, h * HALF:(h + 1) * HALF], ident[0:TT, 0:TT])
                last.then_inc(x_turned, 1)

            def logits(G, h):
                if h == 0:
                    pe.wait_ge(xn_ok, ONE + 2 * G + 2)
                    pe.wait_ge(l_kept, ONE + G)
                last = mm(P[0:LOGITS, 2, 0:CT], wa_s[:, h, :], xn[:, h, :], start=(h == 0), stop=(h == 1))
                if h == 1:
                    last.then_inc(l_mm, 1)

            def values(G, m, h):
                last = mm(P[0:HALF, m, 0:CT], wv_s[:, h, m * HALF:(m + 1) * HALF], xn[:, h, :],
                          start=(h == 0), stop=(h == 1))
                if h == 1:
                    last.then_inc(v_mm, 1)

            def turn_logits(G):
                pe.wait_ge(l_kept, ONE + G + 1)
                pe.wait_ge(s_sub, ONE + G)
                for t in range(NT):
                    last = turn(P[0:TT, 3, t * LP:(t + 1) * LP], lg[:, t * TT:(t + 1) * TT],
                                ident[0:LP, 0:LP])
                last.then_inc(l_turned, 1)

            def turn_weights(G):
                pe.wait_ge(sp_low, ONE + G + 1)
                pe.wait_ge(a_kept, ONE + G)
                bank = P[0:HK * SPLITS, 4, :].bitcast(BF16)
                for h in range(2):
                    for t in range(NT):
                        last = turn(bank[:, h * CT + t * TT:h * CT + (t + 1) * TT],
                                    asp[:, 2 * t + h, :, :].rearrange("p s k -> p (s k)"),
                                    identb[0:TT, 0:TT])
                last.then_inc(a_turned, 1)

            def first_logits(G):
                logits(G, 0)
                logits(G, 1)

            def first_values(G):
                values(G, 0, 0)
                values(G, 0, 1)
                turn_logits(G)

            def first_weights(G, between=(None,) * 3):
                for n in range(3):
                    if n < 2:
                        values(G, 1, n)
                    if between[n]:
                        between[n]()
                stay_warm(8)
                turn_weights(G)
                stay_warm(6)

            for c in range(CHUNKS):
                slot = c % 2
                pe.wait_ge(x_in[slot], ONE + 16 * (c // 2 + 1))
                for h in range(2):
                    if c > 0:
                        pe.wait_ge(x_kept, ONE + 2 * (c - 1) + h + 1)
                    turn_x(h, slot)
            for h in range(2):
                pe.wait_ge(x_kept, ONE + 2 * (CHUNKS - 1) + h + 1)
            group_means(0, G1_BANK)
            group_variances(0, G1_BANK)
            stay_warm(6)
            first_logits(0)
            first_values(0)
            first_weights(0)

            with pe.Fori(0, B) as i:
                def project(G, c, m, part):
                    if part == 0:
                        mm(P[0:HALF, m, 0:CT], ident[0:HALF, 0:HALF], xa[:, m, bass.ds(c * ROWS, ROWS), 0:W],
                           start=True, stop=False)
                    else:
                        if m == 0:
                            pe.wait_ge(padd_ok, ONE + 2 * PADD * G + PADD * part)
                        last = mm(P[0:HALF, m, 0:CT], wp_s[:, part - 1, m * HALF:(m + 1) * HALF],
                                  y0[:, part - 1, :], start=False, stop=(part == 2))
                        if part == 2:
                            last.then_inc(o_mm, 1)

                def outlook(c, first, last_chunk):
                    G = CHUNKS * i + c
                    side = []

                    def prepare_next():
                        return [lambda: (logits(G + 1, 0), logits(G + 1, 1)),
                                lambda: (pe.wait_ge(x1_kept, ONE + (2 * G if first else 2 * G - 2)),
                                         values(G + 1, 0, 0)),
                                lambda: turn_logits(G + 1), lambda: values(G + 1, 0, 1),
                                lambda: values(G + 1, 1, 0), lambda: values(G + 1, 1, 1)]
                    if not last_chunk:
                        side += prepare_next()
                    if not first:
                        for m in range(2):
                            for part in range(3):
                                def step(m=m, part=part):
                                    if part == 0:
                                        if not last_chunk:
                                            pe.wait_ge(v_kept, ONE + 2 * (G + 1) + m + 1)
                                    project(G - 1, c - 1, m, part)
                                slot = PROJECT_SLOTS[3 * m + part]
                                side += [None] * (slot - len(side)) + [step]
                    side += [None] * (REPS - len(side))
                    if not last_chunk:
                        side[13] = lambda: turn_weights(G + 1)
                    filler = range(6 if first or last_chunk else 12, REPS)
                    if not first:
                        pe.wait_ge(prod_ok, ONE + REPS * G - 2)
                        stay_warm(5, 5)
                    pe.wait_ge(a_kept, ONE + G + 1)
                    par = (c % 2) * 2 * CT
                    for h in range(2):
                        src = at[:, bass.ds(par + h * CT, CT)]
                        for k in range(KK):
                            n = h * KK + k
                            if n >= 3:
                                pe.wait_ge(prod_ok, ONE + REPS * G + n - 2)
                            elif first:
                                pe.wait_ge(prod_ok, ONE + REPS * G)
                            else:
                                pe.wait_ge(prod_ok, ONE + REPS * G + n - 2)
                            if n in filler:
                                stay_warm(1, 5 + n % 3)
                            mm(P[0:HALF, 5 + n % 3, 0:CT], sel[:, k, :], src, start=True, stop=True
                               ).then_inc(rep_mm, 1)
                            if side[n]:
                                side[n]()

                G0 = CHUNKS * i
                pe.wait_ge(v_kept, ONE + 2 * G0 + 2)
                outlook(0, True, False)
                with pe.Fori(1, CHUNKS - 1) as c:
                    outlook(c, False, False)
                outlook(CHUNKS - 1, False, True)
                pe.wait_ge(x1_kept, ONE + 2 * (G0 + CHUNKS - 1))
                for part in range(3):
                    if part == 2:
                        pe.wait_ge(prod_ok, ONE + REPS * (G0 + CHUNKS))
                        stay_warm(16)
                    for m in range(2):
                        project(G0 + CHUNKS - 1, CHUNKS - 1, m, part)
                stay_warm(6)
                group_means(2 * i + 1, G2_BANK)
                stay_warm(3)
                group_variances(2 * i + 1, G2_BANK)
                stay_warm(10)

                def qkv(w, par, j):
                    R = NW * i + w
                    if j == 0:
                        pe.wait_ge(xw_ok, ONE + 2 * R + 2)
                    if j >= 2:
                        pe.wait_ge(qkv_kept, ONE + QKV * R + j - 1)
                    elif not (isinstance(w, int) and w == 0):
                        pe.wait_ge(qkv_kept, ONE + QKV * R + j - 1)
                        if not (isinstance(w, int) and w == 1):
                            pe.wait_ge(x_kept, ONE + 2 * (CHUNKS * (i + 1) + w - 3) + j + 1)
                    for h in range(2):
                        if j < 4:
                            col = C * (1 - j // 2) + (j % 2) * HALF
                            last = mm(P[0:HALF, j % 2, 0:RT], wt[:, h, col:col + HALF], xw[:, par, h, :],
                                      start=(h == 0), stop=(h == 1))
                        else:
                            p = j - 4
                            last = mm(P[0:2 * N, j % 2, 0:C], xw[:, par, h, p * 2 * N:(p + 1) * 2 * N],
                                      wt[:, h, 2 * C:3 * C], start=(h == 0), stop=(h == 1))
                    last.then_inc(qkv_mm, 1)

                def scores(w, par, p):
                    R = NW * i + w
                    Q = PAIRS * R + p
                    if p % 2 == 0:
                        pe.wait_ge(k_in[p // 2], ONE + 16 * BDMA * (R + 1))
                    if p == 0:
                        pe.wait_ge(qkv_kept, ONE + QKV * R + 4)
                    for h in range(2):
                        if not (isinstance(w, int) and w == 0 and p == 0):
                            pe.wait_ge(t_add, ONE + 2 * Q + h - 1)
                        for s in range(2):
                            win = 2 * p + s
                            col = (win * N) % (RT // 2)
                            last = mm(P[s * SLOT:(s + 1) * SLOT, 2 + h, 0:HH * N],
                                      qs[:, par, h, win * N:win * N + SLOT],
                                      kbd[:, p // 2, h, :, col:col + N], start=True, stop=True)
                        last.then_inc(sc_mm, 1)

                def turn_probs(w, p):
                    Q = PAIRS * (NW * i + w) + p
                    pe.wait_ge(p_norm, ONE + Q + 1)
                    for b in range(2):
                        if not (isinstance(w, int) and w == 0 and p == 0):
                            pe.wait_ge(p_kept, ONE + 2 * Q + b - 1)
                        for c in range(3):
                            hp = 3 * b + c
                            last = turn(P[0:2 * N, 4 + b, c * 128:(c + 1) * 128],
                                        ps_[:, p % 2, hp * 2 * N:(hp + 1) * 2 * N], ident[:])
                        last.then_inc(p_turned, 1)

                def attend(w, par, p):
                    R = NW * i + w
                    Q = PAIRS * R + p
                    if p == 0:
                        pe.wait_ge(v_in, ONE + 64 * (R + 1))
                    pe.wait_ge(p_kept, ONE + 2 * Q + 2)
                    pe.wait_ge(y_kept, ONE + Q)
                    for hp in range(NH // 2):
                        for s in range(2):
                            col = (hp // 3) * 2 * N + s * N
                            r0 = 32 * (hp % 3)
                            last = mm(P[r0:r0 + 32, 6, col:col + N],
                                      vbd[:, par, 2 * p + s, 2 * HD * hp:2 * HD * (hp + 1)],
                                      pt[:, p % 2, hp, s, :], start=True, stop=True)
                    last.then_inc(y_mm, 1)

                def project_out(w, par, p):
                    R = NW * i + w
                    n = min(TT, RT - TT * p)
                    if p == 0:
                        pe.wait_ge(y_kept, ONE + PAIRS * (R + 1))
                        pe.wait_ge(xr_ok, ONE + 2 * (R + 1))
                    pe.wait_ge(out_ok, ONE + PAIRS * R + p)
                    for h in range(2):
                        last = mm(P[0:n, 7, 0:C], yt[:, par, h, p * TT:p * TT + n], wot[:, h, :],
                                  start=(h == 0), stop=(h == 1))
                    for h in range(2):
                        last = turn(P[0:n, 7, C + h * HALF:C + (h + 1) * HALF], xr[:, par, h, p * TT:p * TT + n],
                                    ident[0:HALF, 0:HALF])
                    last.then_inc(out_mm, 1)

                def turn_next(w, par, half, last_row):
                    R = NW * i + w
                    slot = 1 - par
                    pe.wait_ge(x_in[slot], ONE + 16 * ((4 - slot) * (i + 1) + half + 1))
                    pe.wait_ge(qkv_kept, ONE + QKV * (R + (1 if last_row else 2)))
                    if last_row:
                        pe.wait_ge(x_kept, ONE + 2 * (CHUNKS * (i + 2) - 1))
                    for h in range(2):
                        turn_x(h, slot)

                def window_row(w, par, first, last_row, half=None):
                    for p in range(PAIRS):
                        turn_probs(w, p)
                        if p < 2:
                            scores(w, par, p + 2)
                        elif not last_row:
                            scores(w + 1, 1 - par, p - 2)
                        if not last_row:
                            for j in STEP_TILES[p]:
                                qkv(w + 1, 1 - par, j)
                        if p == (TURN_LAST if last_row else PAIRS - 1) and not first:
                            turn_next(w, par, half, last_row)
                        if last_row and p == 1:
                            pe.wait_ge(x_kept, ONE + 2 * CHUNKS * (i + 2))
                            group_means(2 * i + 2, G1_BANK)
                        if last_row and p == 2:
                            group_variances(2 * i + 2, G1_BANK)
                        if last_row and p == 3:
                            pe.wait_ge(t_add, ONE + 2 * PAIRS * NW * (i + 1))
                            stay_warm(7, 1)
                            first_logits(CHUNKS * (i + 1))
                        elif last_row:
                            if p == 0:
                                pe.wait_ge(x_kept, ONE + 2 * CHUNKS * (i + 2))
                            stay_warm(3, 1)
                        if first and p >= 2:
                            stay_warm(2 if p == 2 else 8)
                        attend(w, par, p)
                        if last_row and p == 3:
                            first_values(CHUNKS * (i + 1))
                        if not first:
                            project_out(w - 1, 1 - par, p)

                for j in range(QKV):
                    qkv(0, 0, j)
                scores(0, 0, 0)
                scores(0, 0, 1)
                stay_warm(20)
                window_row(0, 0, True, False)
                with pe.Fori(0, NW // 2 - 1) as u:
                    window_row(2 * u + 1, 1, False, False, u)
                    window_row(2 * u + 2, 0, False, False, u)
                window_row(NW - 1, 1, False, True, NW // 2 - 1)
                project_out(NW - 1, 1, 0)
                first_weights(CHUNKS * (i + 1), (
                    lambda: project_out(NW - 1, 1, 1),
                    lambda: project_out(NW - 1, 1, 2),
                    lambda: (project_out(NW - 1, 1, 3),
                             pe.wait_ge(out_ok, ONE + PAIRS * NW * (i + 1)))))

        @block.scalar
        def _(act):
            go = nc.scalar.activation
            for b in range(8):
                act.wait_ge(w_turned, b + 1)
                src = P[0:HALF, b % 4, 0:C].rearrange("p (h n) -> p h n", h=2)
                if b < 2:
                    ins = go(wt[:, :, b * HALF:(b + 1) * HALF], src, ACT.Copy, scale=HD ** -0.5)
                elif b < 6:
                    ins = go(wt[:, :, b * HALF:(b + 1) * HALF], src, ACT.Copy)
                else:
                    ins = go(wot[:, :, (b - 6) * HALF:(b - 5) * HALF], src, ACT.Copy)
                ins.then_inc(w_kept, 1)

            def load_table(n, func):
                act.wait_ge(g_table, ONE + n)
                go(table_t[:], eps_s[:], func).then_inc(g_table, 1)

            def deviation(g, bank):
                act.wait_ge(g_var, ONE + g + 1)
                go(gstd[:], P[0:HALF, bank, 2:4], ACT.Sqrt, bias=eps_s[:]).then_inc(g_std, 1)

            act.wait_ge(zeroed, 9)
            act.wait_ge(wscaled, 1)
            act.wait_ge(bout_ok, 1)
            def keep_x(image, c):
                for h in range(2):
                    act.wait_ge(x_turned, ONE + 2 * (CHUNKS * image + c) + h + 1)
                    go(xa[:, h, bass.ds(c * ROWS, ROWS), 0:W],
                       P[0:HALF, h, 0:CT].rearrange("p (r n) -> p r n", n=W), ACT.Copy).then_inc(x_kept, 1)

            def normalize(G, c):
                for h in range(2):
                    if h == 0:
                        act.wait_ge(l_mm, ONE + G)
                        act.wait_ge(v_mm, ONE + 2 * G)
                    go(xn[:, h, :].rearrange("p (r n) -> p r n", n=W), xa[:, h, bass.ds(c * ROWS, ROWS), 0:W],
                       ACT.Identity, bias=gb[:, h:h + 1], scale=ga[:, h:h + 1]).then_inc(xn_ok, 1)

            def keep_logits(G):
                act.wait_ge(l_mm, ONE + G + 1)
                act.wait_ge(l_turned, ONE + G)
                go(lg[0:LOGITS, :], P[0:LOGITS, 2, 0:CT], ACT.Identity, bias=ba_s[:]).then_inc(l_kept, 1)

            def keep_values(G, c, m):
                act.wait_ge(v_mm, ONE + 2 * G + m + 1)
                go(vpad[:, m, bass.ds(c * ROWS + 1, ROWS), 1:W + 1],
                   P[0:HALF, m, 0:CT].rearrange("p (r n) -> p r n", n=W), ACT.Identity,
                   bias=bias[:, 0, m:m + 1]).then_inc(v_kept, 1)

            def exps(G):
                act.wait_ge(s_sub, ONE + G + 1)
                act.wait_ge(s_norm, ONE + G)
                go(sex[:], ssh[:], ACT.Exp).then_inc(s_exp, 1)

            by_half = lambda ap: ap.rearrange("p (n k) -> p n k", k=HK)

            def split_hi(G):
                act.wait_ge(s_norm, ONE + G + 1)
                act.wait_ge(a_turned, ONE + G)
                go(asp[:, :, 0, :], by_half(sa[:]), ACT.Copy).then_inc(sp_hi, 1)

            def split_mid(G):
                act.wait_ge(sp_rest, ONE + G + 1)
                go(asp[:, :, 1, :], by_half(srest[:]), ACT.Copy).then_inc(sp_mid, 1)

            def keep_weights(G, c, clamp):
                act.wait_ge(a_turned, ONE + G + 1)
                act.wait_ge(rep_mm, ONE + (REPS * G if clamp else REPS * (G - 1)))
                go(at[:, bass.ds((c % 2) * 2 * CT, 2 * CT)],
                   P[0:HK * SPLITS, 4, :].bitcast(BF16)[:, 0:2 * CT], ACT.Copy).then_inc(a_kept, 1)

            def first_norm(image, G):
                act.wait_ge(g_ready, ONE + 2 * (2 * image + 1))
                normalize(G, 0)
                load_table(4 * image + 1, ACT.Exp)

            def first_weights(G, between=(None,) * 4):
                exps(G)
                if between[0]:
                    between[0]()
                split_hi(G)
                keep_values(G, 0, 0)
                if between[1]:
                    between[1]()
                split_mid(G)
                keep_values(G, 0, 1)
                for other in between[2:]:
                    if other:
                        other()
                normalize(G + 1, 1)
                keep_weights(G, 0, True)

            for c in range(CHUNKS):
                keep_x(0, c)
            load_table(0, ACT.Sqrt)
            deviation(0, G1_BANK)
            first_norm(0, 0)
            keep_logits(0)
            first_weights(0)

            with act.Fori(0, B) as i:
                def keep_x1(G, c):
                    for m in range(2):
                        act.wait_ge(o_mm, ONE + 2 * G + m + 1)
                        go(xa[:, m, bass.ds(c * ROWS, ROWS), 0:W],
                           P[0:HALF, m, 0:CT].rearrange("p (r n) -> p r n", n=W), ACT.Identity,
                           bias=bias[:, 1, m:m + 1]).then_inc(x1_kept, 1)

                def outlook(c, first, last_chunk):
                    G = CHUNKS * i + c
                    if not last_chunk:
                        keep_logits(G + 1)
                        keep_values(G + 1, c + 1, 0)
                        exps(G + 1)
                        keep_values(G + 1, c + 1, 1)
                        split_hi(G + 1)
                        split_mid(G + 1)
                        if not (isinstance(c, int) and c == CHUNKS - 2):
                            normalize(G + 2, c + 2)
                    if not first:
                        keep_x1(G - 1, c - 1)
                    if not last_chunk:
                        keep_weights(G + 1, c + 1, first)

                G0 = CHUNKS * i
                outlook(0, True, False)
                with act.Fori(1, CHUNKS - 2) as c:
                    outlook(c, False, False)
                outlook(CHUNKS - 2, False, False)
                outlook(CHUNKS - 1, False, True)
                load_table(4 * i + 2, ACT.Sqrt)
                keep_x1(G0 + CHUNKS - 1, CHUNKS - 1)
                act.wait_ge(x1_kept, ONE + 2 * CHUNKS * (i + 1))
                for h in range(2):
                    go(xa[:, h, 0:H, W:XP], xa[:, h, 0:H, 0:SHIFT], ACT.Copy).then_inc(x1_wrap, 1)
                act.wait_ge(x1_wrap, ONE + 4 * i + 2)
                for h in range(2):
                    go(xa[:, h, H:XP, :], xa[:, h, 0:SHIFT, :], ACT.Copy).then_inc(x1_wrap, 1)
                deviation(2 * i + 1, G2_BANK)
                load_table(4 * i + 3, ACT.Exp)

                def keep_qkv(w, par, j):
                    R = NW * i + w
                    act.wait_ge(qkv_mm, ONE + QKV * R + j + 1)
                    if j == 0:
                        for d in range(2):
                            act.wait_ge(k_in[d], ONE + 16 * BDMA * R)
                    if j == 4:
                        act.wait_ge(v_in, ONE + 64 * R)
                    h = j % 2
                    if j < 2:
                        ins = go(ks[:, h, :], P[0:HALF, h, 0:RT], ACT.Identity, bias=bias[:, 3, h:h + 1])
                    elif j < 4:
                        ins = go(qs[:, par, h, 0:RT], P[0:HALF, h, 0:RT], ACT.Identity, bias=bias[:, 6, h:h + 1])
                    else:
                        dst = vs[:, j - 4, :, :].rearrange("p a (c e d) -> p a c e d", e=2, d=HD)
                        src = P[0:2 * N, h, 0:C].rearrange("p (c e d) -> p c e d", e=2, d=HD)
                        go(dst[:, 0, :, 0, :], src[:, :, 0, :], ACT.Copy)
                        ins = go(dst[:, 1, :, 1, :], src[:, :, 1, :], ACT.Copy)
                    ins.then_inc(qkv_kept, 1)

                def exp_pair(w, p):
                    Q = PAIRS * (NW * i + w) + p
                    act.wait_ge(t_sub, ONE + Q + 1)
                    early = isinstance(w, int) and w == 0 and p < 2
                    act.wait_ge(p_turned, ONE + (2 * Q - 2 * p if early else 2 * Q - 2))
                    go(ps_[:, p % 2, :], ts_[:, p % 2, :], ACT.Exp).then_inc(p_exp, 1)

                def keep_probs(w, p):
                    Q = PAIRS * (NW * i + w) + p
                    for b in range(2):
                        act.wait_ge(p_turned, ONE + 2 * Q + b + 1)
                        if b == 0:
                            early = isinstance(w, int) and w == 0 and p < 2
                            act.wait_ge(y_mm, ONE + (Q - p if early else Q - 1))
                        src = P[0:2 * N, 4 + b, 0:384].rearrange("p (c s n) -> p c s n", c=3, s=2)[:, :, :, 0:N]
                        go(pt[:, p % 2, 3 * b:3 * b + 3, :, :], src, ACT.Copy).then_inc(p_kept, 1)

                def keep_residual(w, p):
                    R = NW * i + w
                    n = min(TT, RT - TT * p)
                    act.wait_ge(out_mm, ONE + PAIRS * R + p + 1)
                    act.wait_ge(out_in[p], ONE + 16 * R)
                    go(ot[0:n, p, :], P[0:n, 7, C:2 * C], ACT.Copy).then_inc(res_kept, 1)

                def window_row(w, par, first, last_row):
                    for p in range(PAIRS):
                        if p < 3:
                            exp_pair(w, p + 1)
                        elif not last_row:
                            exp_pair(w + 1, 0)
                        keep_probs(w, p)
                        if not last_row:
                            for j in STEP_TILES[p]:
                                keep_qkv(w + 1, 1 - par, j)
                        if p == (TURN_LAST if last_row else PAIRS - 1) and not first:
                            act.wait_ge(xr_ok, ONE + 2 * (NW * i + w + 1))
                            keep_x(i + 1, w - 1)
                        if last_row and p == 2:
                            load_table(4 * i + 4, ACT.Sqrt)
                            deviation(2 * i + 2, G1_BANK)
                        if last_row and p == 3:
                            first_norm(i + 1, CHUNKS * (i + 1))
                            keep_logits(CHUNKS * (i + 1))
                        if not first:
                            keep_residual(w - 1, p)

                for j in range(QKV):
                    keep_qkv(0, 0, j)
                exp_pair(0, 0)
                window_row(0, 0, True, False)
                with act.Fori(0, NW // 2 - 1) as u:
                    window_row(2 * u + 1, 1, False, False)
                    window_row(2 * u + 2, 0, False, False)
                window_row(NW - 1, 1, False, True)
                first_weights(CHUNKS * (i + 1), [
                    lambda p=p: keep_residual(NW - 1, p) for p in range(PAIRS)])

        @block.vector
        def _(dve):
            tt, ts, red = nc.vector.tensor_tensor, nc.vector.tensor_scalar, nc.vector.tensor_reduce
            nc.vector.memset(ts_[:, 0, :], 0.0).then_inc(rel_zero, 1)
            dve.wait_ge(consts_in, 16 * NCONST)
            nc.vector.tensor_copy(sel[:].rearrange("p k n -> p (k n)"), self32[:]).then_inc(w_cast, 1)
            ts(bias[:, 6, :], bias[:, 2, :], HD ** -0.5, None, ALU.mult).then_inc(wscaled, 1)
            dve.wait_ge(rel_in, 16 * (1 + 2 * WS))
            for v in range(4):
                tt(relb[:, v, :].rearrange("p (h k) -> p h k", h=NH),
                   rel_raw[:, ::-1, :].rearrange("p k h -> p h k"),
                   mask_s[:, v, :].unsqueeze(1).to_broadcast([128, NH, N]), ALU.add).then_inc(rel_ok, 1)
            dve.wait_ge(bout_mm, 1)
            tt(bout[:], P[0:HALF, 4, 0:2], bias[:, 5, :], ALU.add).then_inc(bout_ok, 1)
            dve.wait_ge(rel_ok, 4)
            dve.wait_ge(bout_ok, 1)

            def aggregate(g, stat, n):
                dve.wait_ge(stat, ONE + n)
                nc.vector.memset(fence[:], 0.0).then_inc(g_agg, 1)
                for h in range(2):
                    nc.vector.bn_aggr(mv[:, h, :], stats[:, h, :, :].rearrange("p c s -> p (c s)")).then_inc(g_agg, 1)

            def deviate(g, bank):
                dve.wait_ge(g_agg, ONE + 3 * (g + 1))
                dve.wait_ge(g_mean, ONE + g + 1)
                tt(gdev[:], mv[:, :, 0], P[0:HALF, bank, 0:2], ALU.subtract).then_inc(g_dev, 1)
                nc.vector.tensor_copy(gmean[:], P[0:HALF, bank, 0:2]).then_inc(g_dev, 1)
                dve.wait_ge(g_dev, ONE + 3 * g + 2)
                tt(gdev[:], gdev[:], gdev[:], ALU.mult).then_inc(g_dev, 1)
                dve.wait_ge(g_dev, ONE + 3 * g + 3)
                tt(gsq[:], gdev[:], mv[:, :, 1], ALU.add).then_inc(g_sq, 1)

            def coefficients(g):
                dve.wait_ge(g_std, ONE + g + 1)
                nc.vector.reciprocal(ga[:], gstd[:]).then_inc(g_rstd, 1)
                dve.wait_ge(g_rstd, ONE + g + 1)
                nc.vector.scalar_tensor_tensor(out=gb[:], in0=gmean[:], scalar=-1.0, in1=ga[:],
                                               op0=ALU.mult, op1=ALU.mult).then_inc(g_ready, 2)

            def stat_x(image, c):
                for h in range(2):
                    dve.wait_ge(x_kept, ONE + 2 * (CHUNKS * image + c) + h + 1)
                    nc.vector.bn_stats(stats[:, h, bass.ds(c, 1), :].rearrange("p a s -> p (a s)"),
                                       xa[:, h, bass.ds(c * ROWS, ROWS), 0:W]).then_inc(x_stat, 1)

            by_head = lambda ap: ap.rearrange("p (n k) -> p n k", k=KK)
            by_tile = lambda ap: ap.rearrange("p (t h) -> p t h", t=NT)

            def soft_shift(G):
                dve.wait_ge(l_turned, ONE + G + 1)
                logit = P[0:TT, 3, 0:NT * LP].rearrange("p (t l) -> p t l", t=NT)[:, :, 0:LOGITS].rearrange(
                    "p t (h k) -> p t h k", k=KK)
                red(by_tile(smx[:]), logit, AX.X, ALU.max).then_inc(s_max, 1)
                dve.wait_ge(s_max, ONE + G + 1)
                dve.wait_ge(s_exp, ONE + G)
                tt(ssh[:].rearrange("p (t h k) -> p t h k", t=NT, k=KK), logit,
                   by_tile(smx[:]).unsqueeze(3).to_broadcast([TT, NT, OHEADS, KK]), ALU.subtract).then_inc(s_sub, 1)

            def soft_sum(G):
                dve.wait_ge(s_exp, ONE + G + 1)
                red(ssum[:], by_head(sex[:]), AX.X, ALU.add).then_inc(s_sum, 1)
                dve.wait_ge(s_sum, ONE + G + 1)
                dve.wait_ge(s_norm, ONE + G)
                nc.vector.reciprocal(srec[:], ssum[:]).then_inc(s_rec, 1)

            for c in range(CHUNKS):
                stat_x(0, c)
            aggregate(0, x_stat, 2 * CHUNKS)
            deviate(0, G1_BANK)
            coefficients(0)
            soft_shift(0)
            soft_sum(0)

            with dve.Fori(0, B) as i:
                def stat_x1(G, c):
                    for m in range(2):
                        dve.wait_ge(x1_kept, ONE + 2 * G + m + 1)
                        nc.vector.bn_stats(stats[:, m, bass.ds(c, 1), :].rearrange("p a s -> p (a s)"),
                                           xa[:, m, bass.ds(c * ROWS, ROWS), 0:W]).then_inc(x1_stat, 1)

                def outlook(c, first, last_chunk):
                    G = CHUNKS * i + c
                    own = OWN_LAST if last_chunk else OWN
                    dve.wait_ge(v_kept, ONE + 2 * (G + 1))
                    for h in range(2):
                        for k in range(KK):
                            n = h * KK + k
                            di, dj = k // 3, k % 3
                            dve.wait_ge(rep_mm, ONE + REPS * G + n + 1)
                            if k < RING:
                                dst = prod[:, k, :]
                                if h == 0 and first:
                                    dve.wait_ge(padd_ok, ONE + 2 * PADD * G)
                                else:
                                    before = min(max(k, 1), (OWN[1] if h == 0 else own[0]) - 1)
                                    dve.wait_ge(padd_ok, ONE + 2 * PADD * G + PADD * (h - 1) + before)
                            else:
                                dst = ptail[:, h, k - RING, :]
                                if k == RING and not (first and h == 1):
                                    dve.wait_ge(padd_ok, ONE + 2 * PADD * G - PADD * (0 if first else 1 - h))
                            if di == 2 and dj == 0 and not last_chunk:
                                dve.wait_ge(v_kept, ONE + 2 * (G + 1) + h + 1)
                            tt(dst.rearrange("p (r n) -> p r n", n=W),
                               P[0:HALF, 5 + n % 3, 0:CT].rearrange("p (r n) -> p r n", n=W),
                               vpad[:, h, bass.ds(c * ROWS + di, ROWS), dj:dj + W], ALU.mult).then_inc(prod_ok, 1)
                            if not last_chunk and n == 3:
                                soft_shift(G + 1)
                            if not last_chunk and n == 6:
                                soft_sum(G + 1)
                        dve.wait_ge(prod_ok, ONE + REPS * G + h * KK + KK)
                        rest = [prod[:, k, :] for k in range(own[h], RING)] + [ptail[:, h, 1, :], ptail[:, h, 2, :]]
                        for n, term in enumerate(rest):
                            if n > 0:
                                dve.wait_ge(tail_ok, ONE + tails(i, G) + h * (KK - 1 - own[0]) + n)
                            tt(ptail[:, h, 0, :], ptail[:, h, 0, :], term, ALU.add).then_inc(tail_ok, 1)
                    if not first:
                        stat_x1(G - 1, c - 1)

                G0 = CHUNKS * i
                outlook(0, True, False)
                with dve.Fori(1, CHUNKS - 1) as c:
                    outlook(c, False, False)
                outlook(CHUNKS - 1, False, True)
                stat_x1(G0 + CHUNKS - 1, CHUNKS - 1)
                aggregate(2 * i + 1, x1_stat, 2 * CHUNKS * (i + 1))
                deviate(2 * i + 1, G2_BANK)
                coefficients(2 * i + 1)
                dve.wait_ge(x1_wrap, ONE + 4 * (i + 1))
                dve.wait_ge(g_ready, ONE + 2 * (2 * i + 2))

                def stage_norm(w, par, h):
                    R = NW * i + w
                    dve.wait_ge(qkv_mm, ONE + (QKV * NW * i if isinstance(w, int) and w < 2 else QKV * (R - 1)))
                    rows = xa[:, h, bass.ds(WS * w + SHIFT, WS), SHIFT:XP].rearrange("p r (j c) -> p j r c", c=WS)
                    ts(xw[:, par, h, :].rearrange("p (j r c) -> p j r c", r=WS, c=WS), rows,
                       ga[:, h:h + 1], gb[:, h:h + 1], ALU.mult, ALU.add).then_inc(xw_ok, 1)

                def stage_residual(w, par, h):
                    R = NW * i + w
                    dve.wait_ge(out_mm, ONE + (PAIRS * NW * i if isinstance(w, int) and w < 2 else PAIRS * (R - 1)))
                    ts(xr[:, par, h, :].rearrange("p (r n) -> p r n", n=W),
                       xa[:, h, bass.ds(WS * w + SHIFT, WS), 0:W], bout[:, h:h + 1], None,
                       ALU.add).then_inc(xr_ok, 1)

                def score_max(w, p, bottom):
                    Q = PAIRS * (NW * i + w) + p
                    kind = 2 * bottom + (p == PAIRS - 1)
                    early = isinstance(w, int) and w == 0 and p < 2
                    dve.wait_ge(p_exp, ONE + (Q - p if early else Q - 1))
                    for h in range(2):
                        dve.wait_ge(sc_mm, ONE + 2 * Q + h + 1)
                        cols = slice(h * HH * N, (h + 1) * HH * N)
                        tt(ts_[:, p % 2, cols], P[:, 2 + h, 0:HH * N], relb[:, kind, cols], ALU.add).then_inc(t_add, 1)
                    dve.wait_ge(t_add, ONE + 2 * Q + 2)
                    red(mx[:, p % 2, :], ts_[:, p % 2, :].rearrange("p (h k) -> p h k", h=NH), AX.X,
                        ALU.max).then_inc(t_max, 1)

                def prob_sum(w, p):
                    Q = PAIRS * (NW * i + w) + p
                    early = isinstance(w, int) and w == 0 and p < 2
                    dve.wait_ge(p_norm, ONE + (Q - p if early else Q - 1))
                    dve.wait_ge(p_exp, ONE + Q + 1)
                    red(sm[:, p % 2, :], ps_[:, p % 2, :].rearrange("p (h k) -> p h k", h=NH), AX.X,
                        ALU.add).then_inc(p_sum, 1)
                    dve.wait_ge(p_sum, ONE + Q + 1)
                    nc.vector.reciprocal(rc[:, p % 2, :], sm[:, p % 2, :]).then_inc(p_rec, 1)

                def keep_y(w, par, p):
                    R = NW * i + w
                    Q = PAIRS * R + p
                    dve.wait_ge(y_mm, ONE + Q + 1)
                    if p == 0:
                        dve.wait_ge(out_mm, ONE + (PAIRS * NW * i if isinstance(w, int) and w < 2 else PAIRS * (R - 1)))
                    for h in range(2):
                        src = P[0:HALF, 6, h * 2 * N:(h + 1) * 2 * N].rearrange("p (s r c) -> p s r c", s=2, c=WS)
                        dst = yt[:, par, h, :].rearrange("p (r n) -> p r n", n=W)
                        col = SHIFT + 2 * WS * p
                        if p < PAIRS - 1:
                            last = nc.vector.tensor_copy(
                                dst[:, :, col:col + 2 * WS].rearrange("p r (s c) -> p s r c", s=2), src)
                        else:
                            nc.vector.tensor_copy(dst[:, :, col:col + WS], src[:, 0, :, :])
                            nc.vector.tensor_copy(dst[:, :, col + WS:W], src[:, 1, :, 0:WS - SHIFT])
                            last = nc.vector.tensor_copy(dst[:, :, 0:SHIFT], src[:, 1, :, WS - SHIFT:WS])
                    last.then_inc(y_kept, 1)

                def finish(w, p):
                    R = NW * i + w
                    n = min(TT, RT - TT * p)
                    dve.wait_ge(res_kept, ONE + PAIRS * R + p + 1)
                    tt(ot[0:n, p, :], ot[0:n, p, :], P[0:n, 7, 0:C], ALU.add).then_inc(out_ok, 1)

                def window_row(w, par, first, last_row):
                    bottom = last_row
                    if last_row:
                        stage_residual(w, par, 0)
                        stage_residual(w, par, 1)
                    for p in range(PAIRS):
                        if p < 3:
                            prob_sum(w, p + 1)
                        elif not last_row:
                            prob_sum(w + 1, 0)
                        if p < 2:
                            score_max(w, p + 2, bottom)
                        elif not last_row:
                            score_max(w + 1, p - 2, w == NW - 2 if isinstance(w, int) else False)
                        if last_row and p == 1:
                            deviate(2 * i + 2, G1_BANK)
                        keep_y(w, par, p)
                        if last_row and p == 2:
                            coefficients(2 * i + 2)
                        if last_row and p == 3:
                            soft_shift(CHUNKS * (i + 1))
                        if not first:
                            finish(w - 1, p)
                        if last_row:
                            if p == TURN_LAST:
                                stat_x(i + 1, w - 1)
                                aggregate(2 * i + 2, x_stat, 2 * CHUNKS * (i + 2))
                        elif p == 0 and not (isinstance(w, int) and w == NW - 2):
                            for h in range(2):
                                stage_norm(w + 2, par, h)
                        elif 1 <= p < 3:
                            stage_residual(w, par, p - 1)
                        elif p == 3 and not first:
                            stat_x(i + 1, w - 1)

                for w in range(2):
                    for h in range(2):
                        stage_norm(w, w, h)
                score_max(0, 0, False)
                score_max(0, 1, False)
                prob_sum(0, 0)
                window_row(0, 0, True, False)
                with dve.Fori(0, NW // 2 - 2) as u:
                    window_row(2 * u + 1, 1, False, False)
                    window_row(2 * u + 2, 0, False, False)
                window_row(NW - 3, 1, False, False)
                window_row(NW - 2, 0, False, False)
                window_row(NW - 1, 1, False, True)
                soft_sum(CHUNKS * (i + 1))
                for p in range(PAIRS):
                    finish(NW - 1, p)

        @block.gpsimd
        def _(pool):
            pool.memset(ident[:], 0.0).then_inc(idents, 1)
            pool.wait_ge(idents, 1)
            pool.affine_select(out=ident[:], in_=ident[:], compare_op=ALU.not_equal, fill=1.0, base=0,
                               pattern=[[-1, 128]], channel_multiplier=1).then_inc(idents, 1)
            pool.wait_ge(idents, 2)
            pool.tensor_copy(identb[:], ident[:]).then_inc(idents, 1)
            for s in counted:
                pool.sem_inc(s, ONE)
            pool.memset(kbd[:], 0.0).then_inc(zeroed, 1)
            pool.memset(vbd[:], 0.0).then_inc(zeroed, 1)
            pool.memset(lg[:], 0.0).then_inc(zeroed, 1)
            pool.memset(vs[:], 0.0).then_inc(zeroed, 1)
            pool.memset(vpad[:, 0, :, :], 0.0).then_inc(zeroed, 1)
            pool.memset(vpad[:, 1, :, :], 0.0).then_inc(zeroed, 1)
            pool.memset(qs[:, 0, :, :], 0.0).then_inc(zeroed, 1)
            pool.memset(qs[:, 1, :, :], 0.0).then_inc(zeroed, 1)
            pool.memset(junk[:], 0.0).then_inc(idents, 1)
            pool.memset(eps_s[:], EPS).then_inc(zeroed, 1)
            tt = nc.gpsimd.tensor_tensor
            by_head = lambda ap: ap.rearrange("p (n k) -> p n k", k=KK)
            by_half = lambda ap: ap.rearrange("p (n k) -> p n k", k=HK)

            def soft_split(G, step):
                if step == 0:
                    pool.wait_ge(sp_low, ONE + G)
                    pool.wait_ge(s_rec, ONE + G + 1)
                    tt(by_head(sa[:]), by_head(sex[:]),
                       srec[:].unsqueeze(2).to_broadcast([TT, NT * OHEADS, KK]), ALU.mult).then_inc(s_norm, 1)
                elif step == 1:
                    pool.wait_ge(sp_hi, ONE + G + 1)
                    tt(by_half(srest[:]), by_half(sa[:]), asp[:, :, 0, :], ALU.subtract).then_inc(sp_rest, 1)
                else:
                    pool.wait_ge(sp_mid, ONE + G + 1)
                    tt(asp[:, :, 2, :], by_half(srest[:]), asp[:, :, 1, :], ALU.subtract).then_inc(sp_low, 1)

            for step in range(3):
                soft_split(0, step)
            with pool.Fori(0, B) as i:
                def outlook(c, last_chunk):
                    G = CHUNKS * i + c
                    own = OWN_LAST if last_chunk else OWN
                    for h in range(2):
                        A = 2 * PADD * G + PADD * h
                        D = REPS * G + KK * h
                        pool.wait_ge(padd_ok, ONE + A)
                        pool.wait_ge(prod_ok, ONE + D + 2)
                        tt(psum_p[:], prod[:, 0, :], prod[:, 1, :], ALU.add).then_inc(padd_ok, 1)
                        for k in range(2, own[h]):
                            pool.wait_ge(prod_ok, ONE + D + k + 1)
                            pool.wait_ge(padd_ok, ONE + A + k - 1)
                            tt(psum_p[:], psum_p[:], prod[:, k, :], ALU.add
                               ).then_inc(padd_ok, 1 if k < own[h] - 1 else PADD - k)
                            if h == 0 and k >= RING - 3 and not last_chunk:
                                soft_split(G + 1, k - (RING - 3))
                        pool.wait_ge(tail_ok, ONE + tails(i, G) + (KK - 1 - own[0] if h == 0 else 2 * (KK - 1) - sum(own)))
                        pool.wait_ge(padd_ok, ONE + A + PADD - 1)
                        pool.wait_ge(o_mm, ONE + 2 * G)
                        tt(y0[:, h, :], psum_p[:], ptail[:, h, 0, :], ALU.add).then_inc(padd_ok, 1)

                G0 = CHUNKS * i
                outlook(0, False)
                with pool.Fori(1, CHUNKS - 1) as c:
                    outlook(c, False)
                outlook(CHUNKS - 1, True)

                per_head = lambda ap: ap.rearrange("p (h k) -> p h k", h=NH)
                spread = lambda ap: ap.unsqueeze(2).to_broadcast([128, NH, N])

                def shift_pair(w, p):
                    Q = PAIRS * (NW * i + w) + p
                    pool.wait_ge(t_max, ONE + Q + 1)
                    tt(per_head(ts_[:, p % 2, :]), per_head(ts_[:, p % 2, :]), spread(mx[:, p % 2, :]),
                       ALU.subtract).then_inc(t_sub, 1)

                def normalize_pair(w, p):
                    Q = PAIRS * (NW * i + w) + p
                    pool.wait_ge(p_rec, ONE + Q + 1)
                    tt(per_head(ps_[:, p % 2, :]), per_head(ps_[:, p % 2, :]), spread(rc[:, p % 2, :]),
                       ALU.mult).then_inc(p_norm, 1)

                def window_row(w, last_row):
                    for p in range(PAIRS):
                        if p < 3:
                            normalize_pair(w, p + 1)
                        elif not last_row:
                            normalize_pair(w + 1, 0)
                        if p < 2:
                            shift_pair(w, p + 2)
                        elif not last_row:
                            shift_pair(w + 1, p - 2)

                shift_pair(0, 0)
                shift_pair(0, 1)
                normalize_pair(0, 0)
                with pool.Fori(0, NW - 1) as w:
                    window_row(w, False)
                window_row(NW - 1, True)
                for step in range(3):
                    soft_split(CHUNKS * (i + 1), step)


_INS = ["x", "L0_conv_W_attn", "L0_conv_b_attn", "L0_conv_W_v", "L0_conv_b_v", "L0_conv_W_proj",
        "L0_conv_b_proj", "L1_conv_qkv_weight", "L1_conv_qkv_bias", "L1_conv_proj_weight",
        "L1_conv_proj_bias", "L1_conv_rel_pos_bias_table"]


def _constants():
    sel = np.zeros((SPLITS, 3, KK, KK, 3, C // OHEADS), np.float32)
    for h in range(3):
        for k in range(KK):
            sel[:, h, k, k, h, :] = 1.0
    sel = sel.reshape(SPLITS * HK, KK * HALF)
    gmat = np.kron(np.eye(HALF // GROUP), np.full((GROUP, GROUP), 1.0 / GROUP)).astype(np.float32)
    mask = np.zeros((128, 4, N), np.float32)
    pos = np.arange(N)
    for bottom in range(2):
        for right in range(2):
            for s in range(2):
                region = np.zeros(N, np.int64)
                if bottom:
                    region += 2 * (pos // WS >= WS - SHIFT)
                if right and s:
                    region += pos % WS >= WS - SHIFT
                mask[s * SLOT:s * SLOT + N, 2 * bottom + right, :] = np.where(
                    region[:, None] != region[None, :], -100.0, 0.0)
    return {"sel": sel, "gmat": gmat, "mask": mask}


def kernel(**inputs):
    import concourse.bacc as _bacc
    from concourse.bass_utils import run_bass_kernel_spmd as _run

    nc = _bacc.Bacc("TRN2", target_bir_lowering=False, num_devices=1)
    arrays, args = {}, []
    for name in _INS:
        a = np.ascontiguousarray(inputs[name])
        if name == "x":
            a = a.reshape(B * H * W, C)
        arrays[f"in_{name}"] = a
        args.append(nc.dram_tensor(f"in_{name}", a.shape, mybir.dt.from_np(a.dtype), kind="ExternalInput").ap())
    for name, a in _constants().items():
        arrays[f"in_{name}"] = a
        args.append(nc.dram_tensor(f"in_{name}", a.shape, mybir.dt.from_np(a.dtype), kind="ExternalInput").ap())
    args.append(nc.dram_tensor("out", (B * H * W, C), F32, kind="ExternalOutput").ap())
    mixer(nc, *args)
    r = _run(nc, [arrays], core_ids=[0])
    return np.asarray(r.results[0]["out"]).reshape(B, H, W, C)
```
